# Optimizing a Trainium2 kernel written in Bass

```python
import numpy as np
import jax
import jax.numpy as jnp

def _softmax(x, axis=-1):
    return jax.nn.softmax(x, axis=axis)

def _gelu(x):
    return jax.nn.gelu(x, approximate=True)

def _silu(x):
    return jax.nn.silu(x)

def _sigmoid(x):
    return jax.nn.sigmoid(x)

def _layernorm(x, axis=-1, eps=1e-05):
    m = jnp.mean(x, axis=axis, keepdims=True)
    v = jnp.var(x, axis=axis, keepdims=True)
    return (x - m) / jnp.sqrt(v + eps)

def _scatter_add(tgt, idx, src, axis=0):
    return tgt.at[idx].add(src)

def _segment_sum(src, seg, n):
    return jax.ops.segment_sum(src, seg, n)
kernel_name = 'mk_vit_tower_d1_tok_img4096_r4_4b96a3'

def setup_inputs(seed: int=0):
    np.random.seed(seed)
    _w = jnp.asarray

    def _rec_inputs():
        import jax
        import jax.numpy as jnp
        _rk = jax.random.key(seed)
        x = -0.00348982 + 0.707501 * jax.random.normal(jax.random.fold_in(_rk, 1), (16, 128, 64, 2), jnp.float32)
        return x
    x = _rec_inputs()

    def _L0_tok_setup():
        import jax, jax.numpy as jnp
        import numpy as np
        H, N, S, CH, LEN = (128, 64, 128, 1, 1024)

        def _s4d_kernel(log_dt, C, B, inv_A_real, A_imag, L):
            dt = jnp.exp(log_dt)
            Cc = C[..., 0] + 1j * C[..., 1]
            Bc = B[..., 0] + 1j * B[..., 1]
            A = -jnp.exp(inv_A_real) + 1j * A_imag
            rep = H // A.shape[0]
            A = jnp.tile(A, (rep, 1))
            Bc = jnp.tile(Bc, (rep, 1))
            dtA = A * dt[:, None]
            Cc = Bc[None, :, :] * Cc
            Cc = Cc * (jnp.exp(dtA) - 1.0) / A
            ell = jnp.arange(L, dtype=jnp.float32)
            V = jnp.exp(dtA[:, :, None] * ell)
            K = 2.0 * jnp.einsum('chn,hnl->chl', Cc, V).real
            return K.astype(jnp.float32)
        key = jax.random.key(seed)
        k1, k2 = jax.random.split(key, 2)
        log_dt = jax.random.uniform(k1, (H,), minval=float(np.log(0.001)), maxval=float(np.log(0.1))).astype(jnp.float32)
        inv_A_real = jnp.full((S, N), float(np.log(0.5)), dtype=jnp.float32)
        A_imag = jnp.tile((np.pi * jnp.arange(N, dtype=jnp.float32))[None, :], (S, 1))
        B = jnp.stack([jnp.ones((S, N), jnp.float32), jnp.zeros((S, N), jnp.float32)], axis=-1)
        C = (jax.random.normal(k2, (CH, H, N, 2)) * 0.5 ** 0.5).astype(jnp.float32)
        return {'log_dt': log_dt, 'C': C, 'B': B, 'inv_A_real': inv_A_real, 'A_imag': A_imag, 'L': LEN}
    _L0_tok_all = _L0_tok_setup()
    _L0_tok_in = {k: v for k, v in _L0_tok_all.items() if k in ('log_dt', 'B', 'inv_A_real', 'A_imag')}
    del _L0_tok_all

    def _L0_attn_setup():
        import math
        import jax, jax.numpy as jnp
        import numpy as np
        N_HEADS = 32
        ALIBI_BIAS_MAX = 8

        def _alibi_slopes(n_heads, alibi_bias_max=8):
            _n = 2 ** math.ceil(math.log2(n_heads))
            m = jnp.arange(1, _n + 1, dtype=jnp.float32) * (alibi_bias_max / _n)
            slopes = 1.0 / jnp.power(2.0, m)
            if _n != n_heads:
                slopes = jnp.concatenate([slopes[1::2], slopes[::2]])[:n_heads]
            return slopes
        key = jax.random.key(seed)
        k1, k2, k3 = jax.random.split(key, 3)
        B, S, D = (1, 512, 1024)
        x = jax.random.normal(k1, (B, S, D), dtype=jnp.float32)
        w_qkv = jax.random.normal(k2, (3 * D, D), dtype=jnp.float32) * 0.02
        b_qkv = jnp.zeros((3 * D,), dtype=jnp.float32)
        w_out = jax.random.normal(k3, (D, D), dtype=jnp.float32) * 0.02
        b_out = jnp.zeros((D,), dtype=jnp.float32)
        return {'x': x, 'w_qkv': w_qkv, 'b_qkv': b_qkv, 'w_out': w_out, 'b_out': b_out}
    _L0_attn_all = _L0_attn_setup()
    _L0_attn_in = {k: v for k, v in _L0_attn_all.items() if k in ('w_qkv', 'b_qkv', 'w_out', 'b_out')}
    del _L0_attn_all

    def _L0_ffn_setup():
        import jax, jax.numpy as jnp
        import numpy as np
        B, S, D_IN, D_OUT = (2, 512, 1024, 1024)
        E, K, R = (8, 2, 16)
        SCALING = 32.0 / 16.0
        key = jax.random.key(seed)
        ks = jax.random.split(key, 6)
        x = jax.random.normal(ks[0], (B, S, D_IN), dtype=jnp.float32)
        gate_w = jax.random.normal(ks[1], (E, D_IN), dtype=jnp.float32) * 0.02
        base_w = jax.random.normal(ks[2], (D_OUT, D_IN), dtype=jnp.float32) * 0.02
        base_b = jax.random.normal(ks[3], (D_OUT,), dtype=jnp.float32) * 0.02
        lora_A = jax.random.normal(ks[4], (E, R, D_IN), dtype=jnp.float32) * 0.02
        lora_B = jax.random.normal(ks[5], (E, D_OUT, R), dtype=jnp.float32) * 0.02
        return {'x': x, 'gate_w': gate_w, 'base_w': base_w, 'base_b': base_b, 'lora_A': lora_A, 'lora_B': lora_B}
    _L0_ffn_all = _L0_ffn_setup()
    _L0_ffn_in = {k: v for k, v in _L0_ffn_all.items() if k in ('gate_w', 'base_w', 'base_b', 'lora_A', 'lora_B')}
    del _L0_ffn_all
    return {'x': x, 'L0_tok_log_dt': _L0_tok_in['log_dt'], 'L0_tok_B': _L0_tok_in['B'], 'L0_tok_inv_A_real': _L0_tok_in['inv_A_real'], 'L0_tok_A_imag': _L0_tok_in['A_imag'], 'L0_attn_w_qkv': _L0_attn_in['w_qkv'], 'L0_attn_b_qkv': _L0_attn_in['b_qkv'], 'L0_attn_w_out': _L0_attn_in['w_out'], 'L0_attn_b_out': _L0_attn_in['b_out'], 'L0_ffn_gate_w': _L0_ffn_in['gate_w'], 'L0_ffn_base_w': _L0_ffn_in['base_w'], 'L0_ffn_base_b': _L0_ffn_in['base_b'], 'L0_ffn_lora_A': _L0_ffn_in['lora_A'], 'L0_ffn_lora_B': _L0_ffn_in['lora_B']}

def reference(x, L0_tok_log_dt, L0_tok_B, L0_tok_inv_A_real, L0_tok_A_imag, L0_attn_w_qkv, L0_attn_b_qkv, L0_attn_w_out, L0_attn_b_out, L0_ffn_gate_w, L0_ffn_base_w, L0_ffn_base_b, L0_ffn_lora_A, L0_ffn_lora_B):
    import jax
    import jax.numpy as jnp

    def _L0_tok_ref(log_dt, C, B, inv_A_real, A_imag, L):
        import jax, jax.numpy as jnp
        import numpy as np
        H, N, S, CH, LEN = (128, 64, 128, 1, 1024)

        def _s4d_kernel(log_dt, C, B, inv_A_real, A_imag, L):
            dt = jnp.exp(log_dt)
            Cc = C[..., 0] + 1j * C[..., 1]
            Bc = B[..., 0] + 1j * B[..., 1]
            A = -jnp.exp(inv_A_real) + 1j * A_imag
            rep = H // A.shape[0]
            A = jnp.tile(A, (rep, 1))
            Bc = jnp.tile(Bc, (rep, 1))
            dtA = A * dt[:, None]
            Cc = Bc[None, :, :] * Cc
            Cc = Cc * (jnp.exp(dtA) - 1.0) / A
            ell = jnp.arange(L, dtype=jnp.float32)
            V = jnp.exp(dtA[:, :, None] * ell)
            K = 2.0 * jnp.einsum('chn,hnl->chl', Cc, V).real
            return K.astype(jnp.float32)
        return _s4d_kernel(log_dt, C, B, inv_A_real, A_imag, L)

    def _L0_attn_ref(x, w_qkv, b_qkv, w_out, b_out):
        import math
        import jax, jax.numpy as jnp
        import numpy as np
        N_HEADS = 32
        ALIBI_BIAS_MAX = 8

        def _alibi_slopes(n_heads, alibi_bias_max=8):
            _n = 2 ** math.ceil(math.log2(n_heads))
            m = jnp.arange(1, _n + 1, dtype=jnp.float32) * (alibi_bias_max / _n)
            slopes = 1.0 / jnp.power(2.0, m)
            if _n != n_heads:
                slopes = jnp.concatenate([slopes[1::2], slopes[::2]])[:n_heads]
            return slopes
        B, S, D = x.shape
        H = N_HEADS
        hd = D // H
        qkv = jnp.einsum('bsd,od->bso', x, w_qkv) + b_qkv
        q, k, v = jnp.split(qkv, 3, axis=-1)
        q = q.reshape(B, S, H, hd)
        k = k.reshape(B, S, H, hd)
        v = v.reshape(B, S, H, hd)
        scale = 1.0 / math.sqrt(hd)
        scores = jnp.einsum('bqhd,bkhd->bhqk', q, k) * scale
        slopes = _alibi_slopes(H, ALIBI_BIAS_MAX)
        positions = jnp.arange(1 - S, 1, dtype=jnp.float32)
        alibi = slopes[:, None] * positions[None, :]
        scores = scores + alibi[None, :, None, :]
        causal = jnp.arange(S)[:, None] >= jnp.arange(S)[None, :]
        scores = jnp.where(causal[None, None, :, :], scores, jnp.float32(-1000000000.0))
        attn = jax.nn.softmax(scores, axis=-1)
        out = jnp.einsum('bhqk,bkhd->bqhd', attn, v).reshape(B, S, D)
        return jnp.einsum('bsd,od->bso', out, w_out) + b_out

    def _L0_ffn_ref(x, gate_w, base_w, base_b, lora_A, lora_B):
        import jax, jax.numpy as jnp
        import numpy as np
        B, S, D_IN, D_OUT = (2, 512, 1024, 1024)
        E, K, R = (8, 2, 16)
        SCALING = 32.0 / 16.0
        gate_logits = jnp.einsum('bsd,ed->bse', x, gate_w)
        weights, selected = jax.lax.top_k(gate_logits, K)
        weights = jax.nn.softmax(weights.astype(jnp.float32), axis=2).astype(x.dtype)
        result = jnp.einsum('bsd,od->bso', x, base_w) + base_b
        w_full = jnp.sum(jax.nn.one_hot(selected, E, dtype=x.dtype) * weights[..., None], axis=2)
        low = jnp.einsum('bsd,erd->ebsr', x, lora_A)
        lora_out = jnp.einsum('ebsr,eor,bse->bso', low, lora_B, w_full)
        result = result + SCALING * lora_out
        return result
    h = _L0_tok_ref(L0_tok_log_dt, x, L0_tok_B, L0_tok_inv_A_real, L0_tok_A_imag, 1024)
    h = h + _L0_attn_ref(_layernorm(h, axis=-1), L0_attn_w_qkv, L0_attn_b_qkv, L0_attn_w_out, L0_attn_b_out)
    h = h + _L0_ffn_ref(_layernorm(h, axis=-1), L0_ffn_gate_w, L0_ffn_base_w, L0_ffn_base_b, L0_ffn_lora_A, L0_ffn_lora_B)
    return h

_drawn_inputs = setup_inputs


def setup_inputs(seed=0):
    import zlib

    import numpy as np

    out = dict(_drawn_inputs(seed))
    spreads = {'L0_tok_inv_A_real': (-0.6931471824645996, 0.2),
     'L0_attn_b_qkv': (0.0, 0.1),
     'L0_attn_b_out': (0.0, 0.1)}
    factors = {}
    for name, (base, spread) in spreads.items():
        noise = np.random.default_rng([zlib.crc32(name.encode()), seed]).standard_normal(out[name].shape)
        drawn = base * np.exp(spread * noise) if base else spread * noise
        out[name] = jnp.asarray(drawn.astype(out[name].dtype))
    for name, factor in factors.items():
        out[name] = (out[name] * factor).astype(out[name].dtype)
    return out
```

```python
import concourse.bass as bass
from concourse import mybir
from concourse.alu_op_type import AluOpType as ALU
import numpy as np

F32 = mybir.dt.float32
F32R = mybir.dt.float32r
I32 = mybir.dt.int32
ACT = mybir.ActivationFunctionType
AX = mybir.AxisListType

P = 128
BATCH, SEQ, NSTATE = 16, 128, 64
DM = 1024
DK = DM // P
TOK = BATCH * SEQ
NHEAD, HD = 32, 32
HG = P // HD
NG = NHEAD // HG
TB = 512
NTB = TOK // TB
CB = TB // SEQ
NE, RANK = 8, 16
QK_SCALE = 1.0 / float(np.sqrt(HD))
LORA_SCALE = 32.0 / 16.0
LN_EPS = 1e-5

NA, NI, NJ = DM // P, 8, 16
NF = NA + NI + NJ
SU = 8

CONST_AT = 16512
CONST_BYTES = 1536
X_AT = CONST_AT + CONST_BYTES
X_BYTES = 2 * DK * TOK * 4
H_AT = X_AT + X_BYTES
H_BYTES = DK * TOK * 4
T_AT = H_AT + H_BYTES
END_AT = 229368


class Region:

    def __init__(self, nc, tag, start, end):
        self.nc, self.tag, self.at, self.end = nc, tag, start, end

    def __call__(self, name, shape, dtype=F32):
        size = 4
        for n in shape[1:]:
            size *= n
        t = self.nc.alloc_sbuf_tensor_at(self.tag + name, list(shape), dtype, offset=self.at)
        self.at += (size + 31) // 32 * 32
        assert self.at <= self.end, (name, self.at, self.end)
        return t


def spread(ap, dim, n):
    shape = list(ap.shape)
    shape.insert(dim, n)
    return ap.unsqueeze(dim).broadcast_to(shape)


def constants(nc, sem, ident, mean_w):
    made = sem("constants_made")
    with nc.Block() as block:
        @block.gpsimd
        def _(pool):
            nc.gpsimd.memset(ident[:, :], 0.0).then_inc(made, 1)
            nc.gpsimd.memset(mean_w[:, :], 1.0 / DM)
            pool.wait_ge(made, 1)
            nc.gpsimd.affine_select(out=ident[:, :], in_=ident[:, :], compare_op=ALU.not_equal, fill=1.0,
                                    base=0, pattern=[[-1, P]], channel_multiplier=1)


def s4d_stage(nc, sem, psum, x, log_dt, b_ri, inv_a, a_imag, ident, H):
    R = Region(nc, "s4_", X_AT, X_AT + X_BYTES)
    T = Region(nc, "s4t_", T_AT, END_AT)
    X1, X2, V1, V2, U1, U2, Y1, Y2 = 0, 16, 32, 48, 64, 72, 80, 88
    NT = 96
    FT = R("factorsT", [P, NT, SEQ])
    mark = R.at
    xr = R("x", [P, BATCH, NSTATE, 2])
    xs = R("x_im_re", [P, BATCH, NSTATE, 2])
    turns = R("turns", [P, 2, NF, NSTATE])
    near = R("near", [P, 2, NF, NSTATE])
    decay = R("decay", [P, NF, NSTATE])
    HR = Region(nc, "s4h_", H_AT, H_AT + H_BYTES)
    fac = HR("factors", [P, NF, NSTATE, 2])
    vv = HR("v", [P, 2, NJ, NSTATE, 2])
    u2 = HR("u2", [P, NI, NSTATE, 2])
    y1 = HR("y1", [P, NA, NSTATE, 2])
    y2 = HR("y2", [P, NA, NSTATE, 2])
    gt = HR("gt", [P, 2, NA, NSTATE])
    ea = HR("exp_in", [P, 2 * NSTATE + 1])
    em = [HR(f"em{k}", [P, 2 * NSTATE + 1]) for k in range(7)]
    emi = HR("emi", [P, 2 * NSTATE + 1], I32)
    bri = HR("b", [P, NSTATE, 2])
    aim = HR("a_imag", [P, NSTATE])
    c = [HR(f"c{k}", [P, NSTATE]) for k in range(24)]
    mi = HR("mult_i", [P, NF], I32)
    mf = HR("mult", [P, NF])

    loaded, iotas = sem("s4_loaded"), sem("s4_iotas")
    chain, trig, trig_in = sem("s4_chain"), sem("s4_trig"), sem("s4_trig_in")
    swapped, doubled, ready, tposed, evac = sem("s4_swapped"), sem("s4_doubled"), sem("s4_ready"), sem("s4_tposed"), [sem("s4_evacA"), sem("s4_evacD")]
    ROUND = 1.5 * 2.0 ** 23
    sig, th, u, ar, expm1 = c[0], c[1], c[2], c[3], c[4]

    with nc.Block() as block:
        @block.sync
        def _(sp):
            sp.dma_start(ea[:, 0:NSTATE], inv_a).then_inc(loaded, 16)
            sp.dma_start(ea[:, NSTATE:NSTATE + 1], log_dt.rearrange("(s o) -> s o", o=1)).then_inc(loaded, 16)
            sp.dma_start(aim[:, :], a_imag).then_inc(loaded, 16)
            sp.dma_start(bri[:, :, :], b_ri).then_inc(loaded, 16)
            sp.dma_start(xr[:, :, :, :], x.rearrange("b s n r -> s b n r")).then_inc(loaded, 16)

        @block.gpsimd
        def _(pool):
            nc.gpsimd.iota(mi[:, 0:NA], pattern=[[P, NA]], base=0, channel_multiplier=0).then_inc(iotas, 1)
            nc.gpsimd.iota(mi[:, NA:NA + NI], pattern=[[NJ, NI]], base=0, channel_multiplier=0).then_inc(iotas, 1)
            nc.gpsimd.iota(mi[:, NA + NI:NF], pattern=[[1, NJ]], base=0, channel_multiplier=0).then_inc(iotas, 1)

        @block.vector
        def _(dve):
            steps = [0]

            def link(ins):
                steps[0] += 1
                ins.then_inc(chain, 1)
                dve.wait_ge(chain, steps[0])

            tt, ts, stt = nc.vector.tensor_tensor, nc.vector.tensor_scalar, nc.vector.scalar_tensor_tensor

            def exact_exp(dst, dst_m1, src, n):
                v, k, r, p, s = (em[q][:, 0:n] for q in range(5))
                link(ts(v, src, -87.0, 88.0, ALU.max, ALU.min))
                link(ts(k, v, float(np.log2(np.e)), ROUND, ALU.mult, ALU.add))
                link(ts(k, k, ROUND, None, ALU.subtract))
                link(stt(r, k, -0.693145751953125, v, ALU.mult, ALU.add))
                link(stt(r, k, -1.42860682030941723e-6, r, ALU.mult, ALU.add))
                link(ts(p, r, 1.0 / 40320, None, ALU.mult))
                for q in (5040, 720, 120, 24, 6, 2, 1):
                    link(stt(p, p, 1.0 / q, r, ALU.add, ALU.mult))
                link(ts(emi[:, 0:n], k, 127.0, 2.0 ** 23, ALU.add, ALU.mult))
                two_k = emi[:, 0:n].bitcast(F32)
                link(ts(s, two_k, 1.0, None, ALU.subtract))
                link(tt(p, p, two_k, ALU.mult))
                link(tt(dst_m1, p, s, ALU.add))
                if dst is not None:
                    link(tt(dst, p, two_k, ALU.add))

            dve.wait_ge(iotas, 3)
            link(nc.vector.tensor_copy(mf[:, :], mi[:, :]))
            dve.wait_ge(loaded, 80)
            exact_exp(em[5][:, 0:NSTATE + 1], em[6][:, 0:NSTATE + 1], ea[:, 0:NSTATE + 1], NSTATE + 1)
            dt = em[5][:, NSTATE:NSTATE + 1]
            link(ts(ar[:, :], em[5][:, 0:NSTATE], -1.0, None, ALU.mult))
            link(ts(sig[:, :], ar[:, :], dt, None, ALU.mult))
            link(ts(th[:, :], aim[:, :], dt, None, ALU.mult))
            link(ts(c[5][:, :], th[:, :], 1.0 / (2 * np.pi), ROUND, ALU.mult, ALU.add))
            link(ts(c[5][:, :], c[5][:, :], ROUND, None, ALU.subtract))
            link(stt(c[6][:, :], c[5][:, :], -6.28125, th[:, :], ALU.mult, ALU.add))
            link(stt(c[6][:, :], c[5][:, :], -(2 * np.pi - 6.28125), c[6][:, :], ALU.mult, ALU.add))
            link(ts(u[:, :], c[6][:, :], 1.0 / (2 * np.pi), None, ALU.mult))
            link(tt(turns[:, 1, :, :], spread(u[:, :], 1, NF), spread(mf[:, :], 2, NSTATE), ALU.mult))
            link(ts(turns[:, 0, :, :], turns[:, 1, :, :], 0.25, None, ALU.add))
            link(ts(near[:, :, :, :], turns[:, :, :, :], ROUND, ROUND, ALU.add, ALU.subtract))
            link(tt(near[:, :, :, :], near[:, :, :, :], turns[:, :, :, :], ALU.subtract))
            link(ts(near[:, :, :, :], near[:, :, :, :], 0.4999999, -0.4999999, ALU.min, ALU.max))
            tt(decay[:, :, :], spread(sig[:, :], 1, NF), spread(mf[:, :], 2, NSTATE), ALU.mult).then_inc(trig_in, 1)
            exact_exp(None, expm1[:, :], sig[:, :], NSTATE)
            dve.wait_ge(trig, 4)
            half, sn = c[7], c[8]
            link(tt(c[9][:, :], half[:, :], half[:, :], ALU.mult))
            link(ts(c[9][:, :], c[9][:, :], -2.0, None, ALU.mult))
            link(ts(c[10][:, :], expm1[:, :], 1.0, None, ALU.add))
            link(tt(c[11][:, :], c[10][:, :], c[9][:, :], ALU.mult))
            link(tt(c[11][:, :], c[11][:, :], expm1[:, :], ALU.add))
            link(tt(c[12][:, :], c[10][:, :], sn[:, :], ALU.mult))
            link(tt(c[13][:, :], ar[:, :], ar[:, :], ALU.mult))
            link(tt(c[14][:, :], aim[:, :], aim[:, :], ALU.mult))
            link(tt(c[13][:, :], c[13][:, :], c[14][:, :], ALU.add))
            link(nc.vector.reciprocal(c[14][:, :], c[13][:, :]))
            link(tt(c[15][:, :], c[11][:, :], ar[:, :], ALU.mult))
            link(tt(c[16][:, :], c[12][:, :], aim[:, :], ALU.mult))
            link(tt(c[15][:, :], c[15][:, :], c[16][:, :], ALU.add))
            link(tt(c[15][:, :], c[15][:, :], c[14][:, :], ALU.mult))
            link(tt(c[16][:, :], c[12][:, :], ar[:, :], ALU.mult))
            link(tt(c[17][:, :], c[11][:, :], aim[:, :], ALU.mult))
            link(tt(c[16][:, :], c[16][:, :], c[17][:, :], ALU.subtract))
            link(tt(c[16][:, :], c[16][:, :], c[14][:, :], ALU.mult))
            link(ts(c[18][:, :], bri[:, :, 0], 2.0, None, ALU.mult))
            link(ts(c[19][:, :], bri[:, :, 1], 2.0, None, ALU.mult))
            link(tt(c[20][:, :], c[15][:, :], c[18][:, :], ALU.mult))
            link(tt(c[21][:, :], c[16][:, :], c[19][:, :], ALU.mult))
            link(tt(c[20][:, :], c[20][:, :], c[21][:, :], ALU.subtract))
            link(tt(c[21][:, :], c[15][:, :], c[19][:, :], ALU.mult))
            link(tt(c[22][:, :], c[16][:, :], c[18][:, :], ALU.mult))
            link(tt(c[21][:, :], c[21][:, :], c[22][:, :], ALU.add))
            gr, gi = c[20], c[21]
            tt(fac[:, :, :, 0], decay[:, :, :], near[:, 0, :, :], ALU.mult)
            link(tt(fac[:, :, :, 1], decay[:, :, :], near[:, 1, :, :], ALU.mult))
            ts(u2[:, :, :, 0], fac[:, NA:NA + NI, :, 1], -1.0, None, ALU.mult)
            nc.vector.tensor_copy(u2[:, :, :, 1], fac[:, NA:NA + NI, :, 0]).then_inc(ready, 1)
            pr, pi = fac[:, 0:NA, :, 0], fac[:, 0:NA, :, 1]
            GR, GI = spread(gr[:, :], 1, NA), spread(gi[:, :], 1, NA)
            tt(gt[:, 0, :, :], GR, pr, ALU.mult)
            link(tt(gt[:, 1, :, :], GI, pi, ALU.mult))
            link(tt(y1[:, :, :, 0], gt[:, 0, :, :], gt[:, 1, :, :], ALU.subtract))
            ts(y1[:, :, :, 1], y1[:, :, :, 0], -1.0, None, ALU.mult)
            tt(gt[:, 0, :, :], GR, pi, ALU.mult)
            link(tt(gt[:, 1, :, :], GI, pr, ALU.mult))
            link(stt(y2[:, :, :, 0], gt[:, 0, :, :], -1.0, gt[:, 1, :, :], ALU.mult, ALU.subtract))
            nc.vector.tensor_copy(y2[:, :, :, 1], y2[:, :, :, 0]).then_inc(ready, 1)
            for g in range(1, NT // 4, 2):
                dve.wait_ge(tposed, g + 1)
                nc.vector.tensor_copy(FT[:, 4 * g:4 * g + 4, :], psum[g % 8][:, 0:512]).then_inc(evac[1], 1)

        @block.scalar
        def _(act):
            act.wait_ge(loaded, 80)
            nc.scalar.copy(xs[:, :, :, 0], xr[:, :, :, 1])
            nc.scalar.copy(xs[:, :, :, 1], xr[:, :, :, 0]).then_inc(swapped, 1)
            act.wait_ge(trig_in, 1)
            nc.scalar.activation(near[:, :, :, :], near[:, :, :, :], ACT.Sin, scale=-2 * np.pi).then_inc(trig, 1)
            nc.scalar.activation(c[7][:, :], u[:, :], ACT.Sin, scale=np.pi).then_inc(trig, 1)
            nc.scalar.activation(c[8][:, :], u[:, :], ACT.Sin, scale=6.283185).then_inc(trig, 1)
            nc.scalar.activation(decay[:, :, :], decay[:, :, :], ACT.Exp).then_inc(trig, 1)
            act.wait_ge(ready, 1)
            for part in range(2):
                ins = nc.scalar.copy(vv[:, part, :, :, :], spread(fac[:, NA + NI:NF, :, part], 3, 2))
            ins.then_inc(doubled, 1)
            for g in range(0, NT // 4, 2):
                act.wait_ge(tposed, g + 1)
                nc.scalar.copy(FT[:, 4 * g:4 * g + 4, :], psum[g % 8][:, 0:512]).then_inc(evac[0], 1)

        @block.tensor
        def _(pe):
            def source(t):
                if t < X2:
                    return xr[:, t, :, :]
                if t < V1:
                    return xs[:, t - X2, :, :]
                if t < U1:
                    return vv[:, (t - V1) // NJ, (t - V1) % NJ, :, :]
                if t < U2:
                    return fac[:, NA + t - U1, :, :]
                if t < Y1:
                    return u2[:, t - U2, :, :]
                if t < Y2:
                    return y1[:, t - Y1, :, :]
                return y2[:, t - Y2, :, :]

            pe.wait_ge(swapped, 1)
            for g in range(NT // 4):
                if 4 * g == V1:
                    pe.wait_ge(doubled, 1)
                if 4 * g == Y1:
                    pe.wait_ge(ready, 2)
                if g >= 8:
                    pe.wait_ge(evac[g % 2], (g - 8) // 2 + 1)
                for t in range(4 * g, 4 * g + 4):
                    ins = nc.tensor.transpose(psum[g % 8][:, (t % 4) * P:(t % 4 + 1) * P], source(t), ident[:, :])
                ins.then_inc(tposed, 1)

    R2 = Region(nc, "s4u_", mark, X_AT + X_BYTES)
    q12 = [R2(f"q12_{k}", [P, 2, SU, P]) for k in range(2)]
    w12 = [R2(f"w12_{k}", [P, 2, SU, BATCH * NA]) for k in range(2)]
    qf = [R2(f"q_{k}", [P, SU, P]) for k in range(2)]
    wf = [R2(f"w_{k}", [P, SU, BATCH * NA]) for k in range(2)]
    parts_w, parts_q, w12_free = sem("s4_parts_w"), sem("s4_parts_q"), sem("s4_w12_free")
    sums, filled, freed = sem("s4_sums"), sem("s4_filled"), sem("s4_freed")
    UNITS = SEQ // SU
    tt = nc.vector.tensor_tensor

    with nc.Block() as block:
        @block.gpsimd
        def _(pool):
            with pool.Fori(0, UNITS // 2) as it:
                for k in range(2):
                    at = bass.ds(it * (2 * SU) + k * SU, SU)
                    pool.wait_ge(w12_free, it * 2 + k + 1)
                    for part, (fx, fy) in enumerate(((X1, Y1), (X2, Y2))):
                        ins = nc.gpsimd.tensor_tensor(
                            out=w12[k][:, part, :, :].rearrange("p s (c a) -> p s c a", a=NA),
                            in0=spread(FT[:, fx:fx + BATCH, at].rearrange("p c s -> p s c"), 3, NA),
                            in1=spread(FT[:, fy:fy + NA, at].rearrange("p a s -> p s a"), 2, BATCH), op=ALU.mult)
                    ins.then_inc(parts_w, 1)

        @block.vector
        def _(dve):
            dve.sem_inc(w12_free, 2)
            with dve.Fori(0, UNITS // 2) as it:
                for k in range(2):
                    at = bass.ds(it * (2 * SU) + k * SU, SU)
                    for part, (fu, fv) in enumerate(((U1, V1), (U2, V2))):
                        ins = tt(q12[k][:, part, :, :].rearrange("p s (i j) -> p s i j", j=NJ),
                                 spread(FT[:, fu:fu + NI, at].rearrange("p i s -> p s i"), 3, NJ),
                                 spread(FT[:, fv:fv + NJ, at].rearrange("p j s -> p s j"), 2, NI), ALU.mult)
                    ins.then_inc(parts_q, 1)
                    dve.wait_ge(freed, it * 2 + k + 1)
                    dve.wait_ge(parts_w, it * 2 + k + 1)
                    tt(wf[k][:, :, :], w12[k][:, 0, :, :], w12[k][:, 1, :, :], ALU.add).then_inc(w12_free, 1)
                    dve.wait_ge(parts_q, it * 2 + k + 1)
                    tt(qf[k][:, :, :], q12[k][:, 0, :, :], q12[k][:, 1, :, :], ALU.add).then_inc(sums, 1)

        @block.tensor
        def _(pe):
            with pe.Fori(0, UNITS // 2) as it:
                for k in range(2):
                    pe.wait_ge(sums, it * 2 + k + 1)
                    pe.wait_ge(freed, it * 2 + k + 1)
                    for s in range(SU):
                        ins = nc.tensor.matmul(psum[2 * k + s // 4][:, (s % 4) * P:(s % 4 + 1) * P],
                                               qf[k][:, s, :], wf[k][:, s, :], start=True, stop=True)
                        if s == 3:
                            ins.then_inc(filled, 1)
                    ins.then_inc(filled, 1)

        @block.scalar
        def _(act):
            act.sem_inc(freed, 2)
            with act.Fori(0, UNITS // 2) as it:
                for k in range(2):
                    for half in range(2):
                        act.wait_ge(filled, it * 4 + 2 * k + half + 1)
                        ins = nc.scalar.copy(
                            H[:, :, :, bass.ds(it * (2 * SU) + k * SU + 4 * half, 4)].rearrange("p a c s -> p s c a"),
                            psum[2 * k + half][:, 0:512].rearrange("p (s c a) -> p s c a", s=4, a=NA))
                    ins.then_inc(freed, 1)


def norm_stage(nc, sem, psum, mean_w, H, XH, XL, h_dram):
    T = Region(nc, "ln_", T_AT, END_AT)
    cen = [T(f"centred{k}", [P, DK, SEQ]) for k in range(2)]
    sums = [T(f"sums{k}", [P, SEQ]) for k in range(2)]
    dev = [T(f"deviation{k}", [P, SEQ]) for k in range(2)]
    rec = [T(f"reciprocal{k}", [P, SEQ]) for k in range(2)]
    nwt = [T(f"newton{k}", [P, SEQ]) for k in range(2)]
    stored = sem("ln_stored")
    summed, averaged, centred, squared, devd = sem("ln_summed"), sem("ln_averaged"), sem("ln_centred"), sem("ln_squared"), sem("ln_devd")
    newton, scaled, high, low = sem("ln_newton"), sem("ln_scaled"), sem("ln_high"), sem("ln_low")
    mean_b, var_b = psum[0:2], psum[2:4]
    tt, ts, stt = nc.vector.tensor_tensor, nc.vector.tensor_scalar, nc.vector.scalar_tensor_tensor

    def square_of(k, half):
        return psum[4 + 2 * k + half][:, 0:512].rearrange("p (a s) -> p a s", s=SEQ)

    with nc.Block() as block:
        @block.sync
        def _(sp):
            for b in range(h_dram.shape[0]):
                sp.dma_start(h_dram[b], H[:, :, 2 * b:2 * b + 2, :]).then_inc(stored, 16)
            sp.wait_ge(stored, 16 * h_dram.shape[0])

        @block.vector
        def _(dve):
            with dve.Fori(0, BATCH // 2) as it:
                def h_of(k):
                    return H[:, :, bass.ds(it * 2 + k, 1), :].rearrange("p a o s -> p a (o s)")

                for k in range(2):
                    nc.vector.tensor_reduce(out=sums[k][:, :], in_=h_of(k).rearrange("p a s -> p s a"), axis=AX.X,
                                            op=ALU.add).then_inc(summed, 1)
                for k in range(2):
                    dve.wait_ge(averaged, it * 4 + k + 1)
                    dve.wait_ge(low, it * 2 + k + 1)
                    tt(cen[k][:, :, :], h_of(k), spread(mean_b[k][:, 0:SEQ], 1, DK), ALU.subtract).then_inc(centred, 1)
                for k in range(2):
                    dve.wait_ge(squared, it * 2 + k + 1)
                    for half in range(2):
                        part = (sums[k] if half == 0 else nwt[k])[:, :]
                        ins = nc.vector.tensor_reduce(out=part, in_=square_of(k, half).rearrange("p a s -> p s a"),
                                                      axis=AX.X, op=ALU.add).then_inc(newton, 1)
                    dve.wait_ge(newton, it * 14 + 2 * k + 2)
                    tt(sums[k][:, :], sums[k][:, :], nwt[k][:, :], ALU.add).then_inc(summed, 1)
                for k in range(2):
                    dve.wait_ge(devd, it * 2 + k + 1)
                    base = it * 14 + 4 + 5 * k
                    nc.vector.reciprocal(rec[k][:, :], dev[k][:, :]).then_inc(newton, 1)
                    dve.wait_ge(newton, base + 1)
                    tt(nwt[k][:, :], rec[k][:, :], rec[k][:, :], ALU.mult).then_inc(newton, 1)
                    dve.wait_ge(newton, base + 2)
                    stt(nwt[k][:, :], var_b[k][:, 0:SEQ], LN_EPS, nwt[k][:, :], ALU.add, ALU.mult).then_inc(newton, 1)
                    dve.wait_ge(newton, base + 3)
                    ts(nwt[k][:, :], nwt[k][:, :], -0.5, 1.5, ALU.mult, ALU.add).then_inc(newton, 1)
                    dve.wait_ge(newton, base + 4)
                    tt(rec[k][:, :], rec[k][:, :], nwt[k][:, :], ALU.mult).then_inc(newton, 1)
                for k in range(2):
                    dve.wait_ge(newton, it * 14 + 9 + 5 * k)
                    tt(cen[k][:, :, :], cen[k][:, :, :], spread(rec[k][:, :], 1, DK), ALU.mult).then_inc(scaled, 1)

        @block.tensor
        def _(pe):
            with pe.Fori(0, BATCH // 2) as it:
                for q, banks in enumerate((mean_b, var_b)):
                    for k in range(2):
                        pe.wait_ge(summed, it * 4 + 2 * q + k + 1)
                        nc.tensor.matmul(banks[k][:, 0:SEQ], mean_w[:, :], sums[k][:, :], start=True, stop=True)\
                            .then_inc(averaged, 1)

        @block.scalar
        def _(act):
            with act.Fori(0, BATCH // 2) as it:
                for k in range(2):
                    act.wait_ge(centred, it * 2 + k + 1)
                    nc.scalar.activation(square_of(k, 0), cen[k][:, 0:DK // 2, :], ACT.Square)
                    nc.scalar.activation(square_of(k, 1), cen[k][:, DK // 2:DK, :], ACT.Square).then_inc(squared, 1)
                for k in range(2):
                    act.wait_ge(averaged, it * 4 + 2 + k + 1)
                    nc.scalar.activation(dev[k][:, :], var_b[k][:, 0:SEQ], ACT.Sqrt, bias=LN_EPS).then_inc(devd, 1)
                for k in range(2):
                    act.wait_ge(scaled, it * 2 + k + 1)
                    nc.scalar.copy(XH[:, :, bass.ds((it * 2 + k) * SEQ, SEQ)], cen[k][:, :, :]).then_inc(high, 1)

        @block.gpsimd
        def _(pool):
            pool.sem_inc(low, 2)
            with pool.Fori(0, BATCH // 2) as it:
                for k in range(2):
                    at = bass.ds((it * 2 + k) * SEQ, SEQ)
                    pool.wait_ge(high, it * 2 + k + 1)
                    nc.gpsimd.tensor_tensor(out=XL[:, :, at], in0=cen[k][:, :, :], in1=XH[:, :, at].bitcast(F32),
                                            op=ALU.subtract).then_inc(low, 1)


Q, V, WA, WB, K, AT, VT = "q", "v", "w first half", "w second half", "k", "attention^T", "v natural"
BANK_OF = {Q: 0, V: 1, WA: 0, WB: 0, K: 1, AT: 0, VT: 1}


class Items:

    def __init__(self):
        self.at, self.n, self.bank_n = {}, 0, [0, 0]

    def add(self, key, kind):
        b = BANK_OF[kind]
        self.at[key, kind] = (self.n, b, self.bank_n[b])
        self.n += 1
        self.bank_n[b] += 1


def attention_stage(nc, sem, psum, ident, XH, XL, w_qkv, b_qkv, attn_dram):
    R = Region(nc, "at_", H_AT, END_AT)
    wh = [R(f"w_high{k}", [P, 3, DK, P], F32R) for k in range(2)]
    wl = [R(f"w_low{k}", [P, 3, DK, P], F32R) for k in range(2)]
    wraw = R("w_raw", [P, DM])
    qT = [R(f"qT{k}", [P, TB]) for k in range(2)]
    kT = [R(f"kT{k}", [P, TB]) for k in range(2)]
    vT = R("vT", [P, TB])
    v1 = R("v_and_one", [P, CB, HG, HD + 1])
    sc = [R(f"scores{k}", [P, HG, SEQ]) for k in range(2)]
    pt = [R(f"probsT{k}", [P, HG, SEQ]) for k in range(2)]
    nbias = R("minus_alibi", [P, HG, SEQ])
    on = R("attended", [P, CB, HG, HD])
    ato = R("attendedT", [P, TB])
    mn = R("minima", [P, 2, HG])
    ri = R("inverse_sums", [P, 2, HG])
    bq = R("biases", [P, NG, 3])
    bg = R("group_biases", [P, 2, 3])
    fence = R("fence", [P, 1])
    S_BANKS, ACC, PT_BANK, PV_BANK = psum[0:4], psum[4:6], psum[6], psum[7]
    tt, ts = nc.vector.tensor_tensor, nc.vector.tensor_scalar
    iot = ato[:, 0:SEQ].bitcast(I32)

    pro, body, last = Items(), Items(), Items()
    for j in range(3):
        pro.add(j, WA)
        pro.add(j, WB)
    for kind in (Q, V, K, VT):
        pro.add(3, kind)
    for its, final in ((body, False), (last, True)):
        for k in range(8):
            ahead = not (final and k == 7)
            wts = k % 4 < 3 and not (final and k >= 4)
            for kind in [Q, V] * ahead + [WA, WB] * wts + [K] * ahead + [AT] + [VT] * ahead:
                its.add(k, kind)
    ITER = NG // 2

    filled = sem("at_acc_filled")
    freed = [sem("at_acc_freed0"), sem("at_acc_freed1")]
    w_loaded, w_high, b_loaded, bias_set, bias_ready = sem("at_w_loaded"), sem("at_w_high"), sem("at_b_loaded"), sem("at_bias_set"), sem("at_bias_ready")
    s_filled, scored, exped, t_filled = sem("at_s_filled"), sem("at_scored"), sem("at_exped"), sem("at_t_filled")
    pt_ready, pv_filled, on_ready, inverted = sem("at_pt_ready"), sem("at_pv_filled"), sem("at_on_ready"), sem("at_inverted")
    stored, halved = sem("at_stored"), sem("at_halved")

    def item(it, key, kind):
        if it is None:
            n, b, r = pro.at[key, kind]
            return b, n, r
        n, b, r = (last if isinstance(it, int) else body).at[key, kind]
        return b, it * body.n + (pro.n + n), it * body.bank_n[b] + (pro.bank_n[b] + r)

    def wait_filled(eng, it, key, kind):
        eng.wait_ge(filled, item(it, key, kind)[1] + 1)

    def wait_freed(eng, it, key, kind):
        b, _, r = item(it, key, kind)
        eng.wait_ge(freed[b], r + 2)

    def wait_bank(eng, it, key, kind):
        b, _, r = item(it, key, kind)
        eng.wait_ge(freed[b], r + 1)

    def bank_of(kind):
        return ACC[BANK_OF[kind]]

    def both(eng, program):
        with eng.Fori(0, ITER - 1) as it:
            program(it)
        program(ITER - 1)

    def weights_ahead(it, k):
        return not (isinstance(it, int) and k >= 4)

    def step_ahead(it, k):
        return not (isinstance(it, int) and k == 7)

    with nc.Block() as block:
        @block.sync
        def _(sp):
            def load(rows):
                sp.dma_start(wraw[:, :], w_qkv[rows, :]).then_inc(w_loaded, 16)

            with nc.allow_non_contiguous_dma("a bias a feature"):
                for j in range(3):
                    sp.dma_start(bq[:, :, j], b_qkv[j * DM:(j + 1) * DM].rearrange("(g p) -> p g", p=P)).then_inc(b_loaded, 16)
            load(slice(0, P))
            for j in range(3):
                wait_filled(sp, None, j, WB)
                if j < 2:
                    load(slice((j + 1) * DM, (j + 1) * DM + P))
                else:
                    load(slice(P, 2 * P))

            def program(it):
                for k in range(8):
                    g, tb = it * 2 + k // 4, k % 4
                    if tb < 3 and weights_ahead(it, k):
                        wait_filled(sp, it, k, WB)
                        j, gn = (tb + 1, g + 1) if tb < 2 else (0, g + 2)
                        if tb < 2 or weights_ahead(it, k + 4):
                            load(bass.ds(gn * P + j * DM, P))
                    wait_freed(sp, it, k, AT)
                    sp.dma_start(attn_dram[bass.ds(g, 1), :, tb * TB:(tb + 1) * TB].rearrange("o p t -> (o p) t"),
                                 ato[:, :]).then_inc(stored, 16)

            both(sp, program)
            sp.wait_ge(stored, 16 * (NG * NTB + 1))

        @block.gpsimd
        def _(pool):
            nc.gpsimd.iota(iot, pattern=[[1, SEQ]], base=1 - SEQ, channel_multiplier=0).then_inc(bias_set, 1)
            pool.wait_ge(bias_set, 2)
            nc.gpsimd.affine_select(out=nbias[:, :, :], in_=nbias[:, :, :], compare_op=ALU.is_ge, fill=1e30,
                                    base=0, pattern=[[0, HG], [-1, SEQ]], channel_multiplier=1).then_inc(bias_set, 1)

        @block.tensor
        def _(pe):
            def weight_transposes(it, key, kind, tile):
                first = 0 if kind == WA else DK // 2
                wait_bank(pe, it, key, kind)
                pe.wait_ge(w_loaded, tile * 16 + 16)
                for d in range(DK // 2):
                    ins = nc.tensor.transpose(bank_of(kind)[:, d * P:(d + 1) * P],
                                              wraw[:, (first + d) * P:(first + d + 1) * P], ident[:, :])
                ins.then_inc(filled, 1)

            def project(it, key, kind, par, tb, a, b):
                j = {Q: 0, K: 1, V: 2}[kind]
                if a == 0:
                    wait_bank(pe, it, key, kind)
                at = slice(tb * TB, (tb + 1) * TB)
                for m in range(a, b):
                    d, part = m // 3, m % 3
                    w, x = ((wl, XH), (wh, XL), (wh, XH))[part]
                    ins = nc.tensor.matmul(bank_of(kind)[:, :], w[par][:, j, d, :], x[:, d, at],
                                           start=(m == 0), stop=(m == 3 * DK - 1))
                if b == 3 * DK:
                    ins.then_inc(filled, 1)

            def v_natural(it, key):
                wait_bank(pe, it, key, VT)
                wait_freed(pe, it, key, V)
                for c in range(CB):
                    ins = nc.tensor.transpose(bank_of(VT)[:, c * P:(c + 1) * P], vT[:, c * P:(c + 1) * P], ident[:, :])
                ins.then_inc(filled, 1)

            for j in range(3):
                weight_transposes(None, j, WA, j)
                weight_transposes(None, j, WB, j)
            wait_freed(pe, None, 2, WA)
            wait_freed(pe, None, 2, WB)
            for kind in (Q, V, K):
                project(None, 3, kind, 0, 0, 0, 3 * DK)
            v_natural(None, 3)

            def program(it):
                for k in range(8):
                    g, tb, n = it * 2 + k // 4, k % 4, it * 8 + k
                    ahead, weights = step_ahead(it, k), tb < 3 and weights_ahead(it, k)
                    par_n, tb_n = (k + 1) // 4 % 2, (k + 1) % 4
                    q, kk = qT[k % 2], kT[k % 2]

                    def proj(kind, a, b):
                        if ahead:
                            project(it, k, kind, par_n, tb_n, a, b)

                    def transposes(c):
                        pe.wait_ge(exped, n * 4 + c + 1)
                        pe.wait_ge(pt_ready, n * 4 + c + 1)
                        for h in range(HG):
                            ins = nc.tensor.transpose(PT_BANK[:, h * P:(h + 1) * P], sc[c % 2][:, h, :], ident[:, :])
                        ins.then_inc(t_filled, 1)

                    def weigh(c):
                        pe.wait_ge(pt_ready, n * 4 + c + 2)
                        pe.wait_ge(on_ready, n * 4 + c + 1)
                        for h in range(HG):
                            ins = nc.tensor.matmul(PV_BANK[:, h * (HD + 1):(h + 1) * (HD + 1)], pt[c % 2][:, h, :],
                                                   v1[:, c, h, :], start=True, stop=True)
                        ins.then_inc(pv_filled, 1)

                    pe.wait_ge(scored, n * 4 + 4)
                    prev = (it, k - 1) if k else ((it - 1, 7) if isinstance(it, int) else None)
                    if k:
                        wait_freed(pe, it, k - 1, Q)
                        wait_freed(pe, it, k - 1, VT)
                    else:
                        pe.wait_ge(freed[0], it * body.bank_n[0] + pro.bank_n[0] + 1)
                        pe.wait_ge(freed[1], it * body.bank_n[1] + pro.bank_n[1] + 1)
                    for c in range(CB):
                        for h in range(HG):
                            rows = slice(h * HD, (h + 1) * HD)
                            ins = nc.tensor.matmul(S_BANKS[h][:, c * P:(c + 1) * P], q[rows, c * P:(c + 1) * P],
                                                   kk[rows, c * P:(c + 1) * P], start=True, stop=True)
                    ins.then_inc(s_filled, 1)
                    if ahead and tb == 3:
                        wait_freed(pe, it, k - 1, WB)
                    proj(Q, 0, 24)
                    transposes(0)
                    proj(V, 0, 8)
                    weigh(0)
                    proj(V, 8, 16)
                    transposes(1)
                    proj(V, 16, 24)
                    weigh(1)
                    if weights:
                        weight_transposes(it, k, WA, (g + 1) * 3 + tb)
                    proj(K, 0, 6)
                    transposes(2)
                    proj(K, 6, 12)
                    weigh(2)
                    if weights:
                        weight_transposes(it, k, WB, (g + 1) * 3 + tb)
                    proj(K, 12, 18)
                    transposes(3)
                    proj(K, 18, 21)
                    weigh(3)
                    proj(K, 21, 24)
                    wait_bank(pe, it, k, AT)
                    pe.wait_ge(on_ready, n * 4 + 5)
                    for c in range(CB):
                        ins = nc.tensor.transpose(bank_of(AT)[:, c * P:(c + 1) * P],
                                                  on[:, c, :, :].rearrange("p h d -> p (h d)"), ident[:, :])
                    ins.then_inc(filled, 1)
                    if ahead:
                        v_natural(it, k)

            both(pe, program)

        @block.scalar
        def _(act):
            act.sem_inc(stored, 16)

            def leave_q(it, key, slot, par):
                wait_filled(act, it, key, Q)
                nc.scalar.activation(qT[slot][:, :], bank_of(Q)[:, :], ACT.Identity, scale=-QK_SCALE,
                                     bias=bg[:, par, 0:1]).then_inc(freed[0], 1)

            def leave_v(it, key, par):
                wait_filled(act, it, key, V)
                nc.scalar.activation(vT[:, :], bank_of(V)[:, :], ACT.Identity, bias=bg[:, par, 2:3]).then_inc(freed[1], 1)

            def leave_k(it, key, slot, par):
                wait_filled(act, it, key, K)
                nc.scalar.activation(kT[slot][:, :], bank_of(K)[:, :], ACT.Identity, bias=bg[:, par, 1:2]).then_inc(freed[1], 1)

            def weights_high(it, key, kind, par, j):
                first = 0 if kind == WA else DK // 2
                wait_filled(act, it, key, kind)
                nc.scalar.copy(wh[par][:, j, first:first + DK // 2, :], bank_of(kind)[:, :]).then_inc(w_high, 1)

            act.sem_inc(freed[0], 1)
            act.sem_inc(freed[1], 1)
            act.wait_ge(b_loaded, 48)
            nc.scalar.activation(bq[:, :, 0], bq[:, :, 0], ACT.Copy, scale=-QK_SCALE).then_inc(bias_ready, 1)
            act.wait_ge(bias_ready, 1)
            nc.scalar.copy(bg[:, 0, :], bq[:, 0, :]).then_inc(bias_ready, 1)
            for j in range(3):
                weights_high(None, j, WA, 0, j)
                weights_high(None, j, WB, 0, j)
            act.wait_ge(bias_ready, 2)
            leave_q(None, 3, 0, 0)
            leave_v(None, 3, 0)
            leave_k(None, 3, 0, 0)

            def program(it):
                for k in range(8):
                    g, tb, n = it * 2 + k // 4, k % 4, it * 8 + k
                    ahead, weights = step_ahead(it, k), tb < 3 and weights_ahead(it, k)
                    par_n = (k // 4 + 1) % 2

                    def exps(c):
                        act.wait_ge(scored, n * 4 + c + 5)
                        for h in range(HG):
                            ins = nc.scalar.activation(sc[c % 2][:, h, :], sc[c % 2][:, h, :], ACT.Exp, scale=-1.0,
                                                       bias=mn[:, c % 2, h:h + 1])
                        ins.then_inc(exped, 1)

                    if ahead and tb == 3:
                        nc.scalar.copy(bg[:, par_n, :], bq[:, bass.ds(g + 1, 1), :].rearrange("p o j -> p (o j)")).then_inc(bias_ready, 1)
                    exps(0)
                    if ahead and tb == 3:
                        act.wait_ge(bias_ready, g + 3)
                    if ahead:
                        leave_q(it, k, (k + 1) % 2, (k + 1) // 4 % 2)
                    exps(1)
                    if ahead:
                        leave_v(it, k, (k + 1) // 4 % 2)
                    exps(2)
                    if weights:
                        weights_high(it, k, WA, par_n, tb)
                    exps(3)
                    if weights:
                        weights_high(it, k, WB, par_n, tb)
                    if ahead:
                        leave_k(it, k, (k + 1) % 2, (k + 1) // 4 % 2)
                    wait_filled(act, it, k, AT)
                    act.wait_ge(stored, n * 16 + 16)
                    nc.scalar.copy(ato[:, :], bank_of(AT)[:, :]).then_inc(freed[0], 1)

            both(act, program)

        @block.vector
        def _(dve):
            def weights_low(it, key, kind, par, j, tile):
                first = 0 if kind == WA else DK // 2
                dve.wait_ge(w_high, tile * 2 + (1 if kind == WA else 2))
                tt(wl[par][:, j, first:first + DK // 2, :], bank_of(kind)[:, :].rearrange("p (d o) -> p d o", o=P),
                   wh[par][:, j, first:first + DK // 2, :].bitcast(F32), ALU.subtract).then_inc(freed[BANK_OF[kind]], 1)

            def leave_v_natural(it, key):
                wait_filled(dve, it, key, VT)
                nc.vector.tensor_copy(v1[:, :, :, 0:HD], bank_of(VT)[:, :].rearrange("p (c h d) -> p c h d", c=CB, h=HG))\
                    .then_inc(freed[1], 1)

            dve.sem_inc(scored, 4)
            dve.sem_inc(pt_ready, 1)
            dve.sem_inc(on_ready, 1)
            nc.vector.memset(v1[:, :, :, HD:HD + 1], 1.0)
            dve.wait_ge(bias_set, 1)
            for h in range(HG):
                slope = float(np.float32(1.0) / np.float32(2.0) ** np.float32((h + 1) * 8.0 / NHEAD))
                ins = ts(nbias[:, h, :], iot, -2.0 * slope, None, ALU.mult)
            ins.then_inc(bias_set, 1)
            for j in range(3):
                weights_low(None, j, WA, 0, j, j)
                weights_low(None, j, WB, 0, j, j)
            leave_v_natural(None, 3)
            dve.wait_ge(bias_set, 3)

            def program(it):
                for k in range(8):
                    g, tb, n = it * 2 + k // 4, k % 4, it * 8 + k
                    ahead, weights = step_ahead(it, k), tb < 3 and weights_ahead(it, k)
                    par_n = (k // 4 + 1) % 2

                    def score(c):
                        for h in range(HG):
                            ins = nc.vector.tensor_tensor_reduce(
                                out=sc[c % 2][:, h, :], in0=S_BANKS[h][:, c * P:(c + 1) * P], in1=nbias[:, h, :],
                                scale=1.0, scalar=3e38, op0=ALU.add, op1=ALU.min, accum_out=mn[:, c % 2, h:h + 1])
                        ins.then_inc(scored, 1)

                    def probs(c):
                        dve.wait_ge(t_filled, n * 4 + c + 1)
                        nc.vector.tensor_copy(pt[c % 2][:, :, :], PT_BANK[:, :].rearrange("p (h q) -> p h q", h=HG))\
                            .then_inc(pt_ready, 1)

                    def normalise(c):
                        dve.wait_ge(pv_filled, n * 4 + c + 1)
                        o = PV_BANK[:, 0:HG * (HD + 1)].rearrange("p (h d) -> p h d", h=HG)
                        nc.vector.reciprocal(ri[:, c % 2, :], o[:, :, HD]).then_inc(inverted, 1)
                        dve.wait_ge(inverted, n * 4 + c + 1)
                        tt(on[:, c, :, :], o[:, :, 0:HD], spread(ri[:, c % 2, :], 2, HD), ALU.mult).then_inc(on_ready, 1)

                    if tb == 0:
                        ts(nbias[:, :, :], nbias[:, :, :], 0.5, None, ALU.mult).then_inc(halved, 1)
                        dve.wait_ge(halved, g + 1)
                    dve.wait_ge(s_filled, n + 1)
                    nc.vector.memset(fence[:, :], 0.0)
                    score(0)
                    score(1)
                    probs(0)
                    score(2)
                    normalise(0)
                    probs(1)
                    score(3)
                    normalise(1)
                    if weights:
                        weights_low(it, k, WA, par_n, tb, (g + 1) * 3 + tb)
                    probs(2)
                    normalise(2)
                    if weights:
                        weights_low(it, k, WB, par_n, tb, (g + 1) * 3 + tb)
                    probs(3)
                    normalise(3)
                    if ahead:
                        leave_v_natural(it, k)

            both(dve, program)


TC = 256
NTC = TOK // TC
TT = TC // P
DT = DM // P


def output_stage(nc, sem, psum, ident, mean_w, h_dram, attn_dram, w_out, b_out, gate_w, base_w, base_b, lora_a, lora_b, out):
    R = Region(nc, "out_", X_AT, END_AT)
    wo_h, wo_l = R("w_out_high", [P, DK, DT, P], F32R), R("w_out_low", [P, DK, DT, P], F32R)
    wb_h, wb_l = R("base_high", [P, DK, DT, P], F32R), R("base_low", [P, DK, DT, P], F32R)
    la_h, la_l = R("lora_a_high", [P, DK, NE * RANK], F32R), R("lora_a_low", [P, DK, NE * RANK], F32R)
    lbT = R("lora_bT", [P, DT, P])
    g_h, g_l = R("gate_high", [P, DK, NE], F32R), R("gate_low", [P, DK, NE], F32R)
    bo, bb = R("b_out", [P, DT]), R("base_b", [P, DT])
    lg, m8 = R("logits", [P, TT, NE]), R("sorted", [P, TT, 8])
    tri = R("earlier", [P, NE, NE])
    pw, rank, wsel = R("pair_weights", [P, 4, TT]), R("rank", [P, TT * NE]), R("selected", [P, 2, TT, NE])
    fence = R("fence", [P, 1])
    blocks_at = R.at
    cen_at = R.at
    atf = R("attended", [P, DK, TC])
    cen = nc.alloc_sbuf_tensor_at("out_centred", [P, DK, TC], F32, offset=cen_at)
    ah, al = R("att_high", [P, DK, TC], F32R), R("att_low", [P, DK, TC], F32R)
    xh = R("norm_high", [P, DK, TC], F32R)
    sq_at = R.at
    xl = R("norm_low", [P, DK, TC], F32R)
    sq = nc.alloc_sbuf_tensor_at("out_squares", [P, DK, TC], F32, offset=sq_at)
    hb = [R(f"h{k}", [P, DK, TC]) for k in range(2)]
    z = R("lora_low", [P, TC])
    y = [R(f"result{k}", [P, TC]) for k in range(2)]
    ost = [R(f"result_natural{k}", [P, TT, 2 * P]) for k in range(2)]
    sums, rec = R("sums", [P, TC]), R("reciprocal", [P, TC])
    nwt = z
    cmp = rec[:, 0:P].rearrange("p (t e j) -> p t e j", t=TT, e=NE)
    eq = rec[:, P:2 * P].rearrange("p (t e j) -> p t e j", t=TT, e=NE)
    wx = rec[:, :].rearrange("p (t e r) -> p t e r", t=TT, e=NE)
    tt, ts, stt = nc.vector.tensor_tensor, nc.vector.tensor_scalar, nc.vector.scalar_tensor_tensor

    W = Region(nc, "outw_", blocks_at, END_AT)
    raw = [W(f"raw{k}", [P, DM]) for k in range(4)]
    raw_la, raw_lb, raw_g = W("raw_lora_a", [P, DM]), W("raw_lora_b", [P, DT, NE, RANK]), W("raw_gate", [NE, DM])
    raw_in = [sem(f"ow_raw_in{k}") for k in range(4)]
    small_in, turned, high, split = sem("ow_small_in"), sem("ow_turned"), sem("ow_high"), sem("ow_split")
    tri_made, lb_out = sem("ow_tri"), sem("ow_lb_out")
    mats = ((w_out, wo_h, wo_l), (base_w, wb_h, wb_l))

    with nc.Block() as block:
        @block.sync
        def _(sp):
            with sp.Fori(0, DT // 2) as it:
                for k in range(4):
                    sp.wait_ge(turned, it * 8 + 2 * k + 2)
                    sp.dma_start(raw[k][:, :], mats[k % 2][0][bass.ds((it * 2 + k // 2) * P, P), :]).then_inc(raw_in[k], 16)

        @block.gpsimd
        def _(pool):
            with nc.allow_non_contiguous_dma("small operands"):
                pool.dma_start(raw_la[:, :], lora_a.rearrange("e r d -> (e r) d")).then_inc(small_in, 16)
                pool.dma_start(raw_g[:, :], gate_w).then_inc(small_in, 16)
                for e in range(NE):
                    pool.dma_start(raw_lb[:, :, e, :], lora_b[e].rearrange("(t p) r -> p t r", p=P)).then_inc(small_in, 16)
                pool.dma_start(bo[:, :], b_out.rearrange("(t p) -> p t", p=P)).then_inc(small_in, 16)
                pool.dma_start(bb[:, :], base_b.rearrange("(t p) -> p t", p=P)).then_inc(small_in, 16)
            nc.gpsimd.memset(tri[:, :, :], 1.0).then_inc(tri_made, 1)
            pool.wait_ge(tri_made, 1)
            nc.gpsimd.affine_select(out=tri[:, :, :], in_=tri[:, :, :], compare_op=ALU.is_gt, fill=0.0, base=0,
                                    pattern=[[1, NE], [-1, NE]], channel_multiplier=0).then_inc(tri_made, 1)
            pool.wait_ge(tri_made, 2)
            pool.wait_ge(small_in, 16 * (NE + 4))

        SMALL = DT * 4

        @block.tensor
        def _(pe):
            pe.sem_inc(turned, 8)
            with pe.Fori(0, DT // 2) as it:
                for k in range(4):
                    pe.wait_ge(raw_in[k], it * 16 + 16)
                    for half in range(2):
                        n = 2 * k + half
                        pe.wait_ge(split, it * 8 + n + 1)
                        for d in range(DK // 2):
                            dk = half * (DK // 2) + d
                            ins = nc.tensor.transpose(psum[n][:, d * P:(d + 1) * P], raw[k][:, dk * P:(dk + 1) * P],
                                                      ident[:, :])
                        ins.then_inc(turned, 1)
            pe.wait_ge(small_in, 16 * (NE + 4))
            for half in range(2):
                pe.wait_ge(split, SMALL + half + 1)
                for d in range(DK // 2):
                    dk = half * (DK // 2) + d
                    ins = nc.tensor.transpose(psum[half][:, d * P:(d + 1) * P], raw_la[:, dk * P:(dk + 1) * P], ident[:, :])
                ins.then_inc(turned, 1)
            pe.wait_ge(split, SMALL + 3)
            for dk in range(DK):
                ins = nc.tensor.transpose(psum[2][:, dk * NE:(dk + 1) * NE], raw_g[:, dk * P:(dk + 1) * P],
                                          ident[0:NE, 0:NE])
            ins.then_inc(turned, 1)
            for half in range(2):
                pe.wait_ge(split, SMALL + 4 + half)
                for t in range(4):
                    ins = nc.tensor.transpose(psum[3 + half][:, t * P:(t + 1) * P],
                                              raw_lb[:, half * 4 + t, :, :], ident[:, :])
                ins.then_inc(turned, 1)

        def halves(h, l, k_half, it=None, k=None):
            d = slice(k_half * (DK // 2), (k_half + 1) * (DK // 2))
            if it is None:
                return h[:, d, :], l[:, d, :]
            at = bass.ds(it * 2 + k // 2, 1)
            return (h[:, d, at, :].rearrange("p d o q -> p d (o q)"), l[:, d, at, :].rearrange("p d o q -> p d (o q)"))

        def as_tiles(bank):
            return bank[:, 0:512].rearrange("p (d o) -> p d o", o=P)

        @block.scalar
        def _(act):
            with act.Fori(0, DT // 2) as it:
                for k in range(4):
                    for half in range(2):
                        n = 2 * k + half
                        act.wait_ge(turned, it * 8 + n + 9)
                        nc.scalar.copy(halves(*mats[k % 2][1:], half, it, k)[0], as_tiles(psum[n])).then_inc(high, 1)
            for half in range(2):
                act.wait_ge(turned, 8 + SMALL + half + 1)
                nc.scalar.copy(halves(la_h, la_l, half)[0], as_tiles(psum[half])).then_inc(high, 1)
            act.wait_ge(turned, 8 + SMALL + 3)
            nc.scalar.copy(g_h[:, :, :], psum[2][:, 0:DK * NE].rearrange("p (d e) -> p d e", e=NE)).then_inc(high, 1)
            for half in range(2):
                act.wait_ge(turned, 8 + SMALL + 4 + half)
                nc.scalar.copy(lbT[:, half * 4:half * 4 + 4, :], as_tiles(psum[3 + half])).then_inc(lb_out, 1)

        @block.vector
        def _(dve):
            dve.sem_inc(split, 8)
            with dve.Fori(0, DT // 2) as it:
                for k in range(4):
                    for half in range(2):
                        n = 2 * k + half
                        dve.wait_ge(high, it * 8 + n + 1)
                        h, l = halves(*mats[k % 2][1:], half, it, k)
                        tt(l, as_tiles(psum[n]), h.bitcast(F32), ALU.subtract).then_inc(split, 1)
            for half in range(2):
                dve.wait_ge(high, SMALL + half + 1)
                h, l = halves(la_h, la_l, half)
                tt(l, as_tiles(psum[half]), h.bitcast(F32), ALU.subtract).then_inc(split, 1)
            dve.wait_ge(high, SMALL + 3)
            tt(g_l[:, :, :], psum[2][:, 0:DK * NE].rearrange("p (d e) -> p d e", e=NE), g_h[:, :, :].bitcast(F32),
               ALU.subtract).then_inc(split, 1)

    ACC, GATE, LOW, TURN, STATS = psum[0:2], psum[2], psum[3], psum[4:6], psum[7]
    at_in, h_in = sem("oc_attended_in"), [sem("oc_h_in0"), sem("oc_h_in1")]
    a_high, a_low = sem("oc_att_high"), sem("oc_att_low")
    filled, freed = sem("oc_acc_filled"), sem("oc_acc_freed")
    summed, averaged, centred, squared, rooted, nstep = sem("oc_summed"), sem("oc_averaged"), sem("oc_centred"), sem("oc_squared"), sem("oc_rooted"), sem("oc_newton")
    scaled, x_high, x_low_p, x_low_d = sem("oc_scaled"), sem("oc_norm_high"), sem("oc_norm_low_pool"), sem("oc_norm_low_dve")
    gated, low_f, low_out = sem("oc_gated"), sem("oc_low_filled"), sem("oc_low_out")
    gstep, diff, expd, wx_ready, wx_turned, z_ready = sem("oc_gate_steps"), sem("oc_diff"), sem("oc_exp"), sem("oc_weights_ready"), sem("oc_weights_turned"), sem("oc_z_ready")
    turned, turn_free = sem("oc_turned"), sem("oc_turn_freed")
    stored = [sem("oc_stored0"), sem("oc_stored1")]
    ITER = NTC // 2
    GATE_STEPS = 12

    def both(eng, program):
        with eng.Fori(0, ITER - 1) as it:
            program(it, False)
        program(ITER - 1, True)

    with nc.Block() as block:
        @block.sync
        def _(sp):
            def load_h(b, slot, half):
                d = slice(half * (DK // 2), (half + 1) * (DK // 2))
                sp.dma_start(hb[slot][:, d, :], h_dram[bass.ds(b, 1), :, d, :, :].rearrange("o p a c s -> p (o a) (c s)"))\
                    .then_inc(h_in[half], 16)

            sp.dma_start(atf[:, :, :], attn_dram[:, :, 0:TC].rearrange("g p t -> p g t")).then_inc(at_in, 16)
            load_h(0, 0, 0)
            load_h(0, 0, 1)
            sp.wait_ge(h_in[0], 16)
            sp.wait_ge(h_in[1], 16)
            load_h(1, 1, 0)
            load_h(1, 1, 1)
            sp.wait_ge(a_high, 1)
            sp.wait_ge(a_low, 1)
            sp.dma_start(atf[:, :, :], attn_dram[:, :, TC:2 * TC].rearrange("g p t -> p g t")).then_inc(at_in, 16)

            def program(it, final):
                for k in range(2):
                    b = it * 2 + k
                    if not final:
                        sp.wait_ge(x_low_p, b + 1)
                        sp.wait_ge(x_low_d, b + 1)
                        sp.dma_start(atf[:, :, :], attn_dram[:, :, bass.ds(b * TC + 2 * TC, TC)].rearrange("g p t -> p g t"))\
                            .then_inc(at_in, 16)
                    for pair in range(DT // 2):
                        if not final and pair % 2 == 0 and pair:
                            sp.wait_ge(freed, b * (2 * DT) + 2 * DT + 4 + 2)
                            load_h(b + 2, k, 0)
                        sp.wait_ge(turn_free, b * (DT // 2) + pair + 3)
                        sp.dma_start(out[bass.ds(b * TC, TC), pair * 2 * P:(pair + 1) * 2 * P]
                                     .rearrange("(t p) o -> p t o", p=P), ost[pair % 2][:, :, :]).then_inc(stored[pair % 2], 16)
                    if not final:
                        load_h(b + 2, k, 1)

            both(sp, program)
            for q in range(2):
                sp.wait_ge(stored[q], 16 * (NTC * DT // 4 + 1))

        @block.tensor
        def _(pe):
            def products(r, w_h, w_l, x_h, x_l, ot, more):
                pe.wait_ge(freed, r + 1)
                bank = ACC[ot % 2][:, 0:TC]
                for m in range(3 * DK):
                    d, part = m // 3, m % 3
                    w, x = ((w_l, x_h), (w_h, x_l), (w_h, x_h))[part]
                    ins = nc.tensor.matmul(bank, w[:, d, ot, :], x[:, d, :], start=(m == 0),
                                           stop=(m == 3 * DK - 1 and not more))
                if not more:
                    ins.then_inc(filled, 1)

            def average(source, count):
                pe.wait_ge(summed, count)
                nc.tensor.matmul(STATS[:, 0:TC], mean_w[:, :], source[:, :], start=True, stop=True).then_inc(averaged, 1)

            pe.sem_inc(turned, 2)
            pe.wait_ge(a_low, 1)
            for ot in range(DT):
                products(ot, wo_h, wo_l, ah, al, ot, False)
            average(sums, 1)

            def program(it, final):
                for k in range(2):
                    b = it * 2 + k
                    ahead = not (final and k == 1)
                    r0 = b * (2 * DT) + DT
                    if ahead:
                        pe.wait_ge(a_low, b + 2)
                        for ot in range(3):
                            products(r0 + ot, wo_h, wo_l, ah, al, ot, False)
                    average(sums, b * 2 + 2)
                    if ahead:
                        for ot in range(3, DT):
                            products(r0 + ot, wo_h, wo_l, ah, al, ot, False)
                        r0 = r0 + DT
                    pe.wait_ge(x_low_p, b + 1)
                    pe.wait_ge(x_low_d, b + 1)
                    for t in range(TT):
                        for m in range(3 * DK):
                            d, part = m // 3, m % 3
                            x, w = ((xh, g_l), (xl, g_h), (xh, g_h))[part]
                            ins = nc.tensor.matmul(GATE[:, t * NE:(t + 1) * NE], x[:, d, t * P:(t + 1) * P], w[:, d, :],
                                                   start=(m == 0), stop=(m == 3 * DK - 1))
                    ins.then_inc(gated, 1)
                    for m in range(3 * DK):
                        d, part = m // 3, m % 3
                        w, x = ((la_l, xh), (la_h, xl), (la_h, xh))[part]
                        ins = nc.tensor.matmul(LOW[:, 0:TC], w[:, d, :], x[:, d, :], start=(m == 0), stop=(m == 3 * DK - 1))
                    ins.then_inc(low_f, 1)

                    def lora(ot):
                        nc.tensor.matmul(ACC[ot % 2][:, 0:TC], lbT[:, ot, :], z[:, :], start=False, stop=True).then_inc(filled, 1)

                    def turn(ot):
                        pe.wait_ge(freed, r0 + ot + 3)
                        if ot % 2 == 0:
                            pe.wait_ge(turn_free, b * (DT // 2) + ot // 2 + 1)
                        for t in range(TT):
                            ins = nc.tensor.transpose(TURN[ot // 2 % 2][:, t * 2 * P + (ot % 2) * P:t * 2 * P + (ot % 2 + 1) * P],
                                                      y[ot % 2][:, t * P:(t + 1) * P], ident[:, :])
                        ins.then_inc(turned, 1)

                    for ot in range(2):
                        products(r0 + ot, wb_h, wb_l, xh, xl, ot, True)
                    pe.wait_ge(wx_ready, b + 1)
                    for t in range(TT):
                        ins = nc.tensor.transpose(GATE[:, P + t * P:P + (t + 1) * P], rec[:, t * P:(t + 1) * P], ident[:, :])
                    ins.then_inc(wx_turned, 1)
                    pe.wait_ge(z_ready, b + 1)
                    lora(0)
                    lora(1)
                    for ot in range(2, DT):
                        products(r0 + ot, wb_h, wb_l, xh, xl, ot, True)
                        lora(ot)
                        turn(ot - 2)
                        if ot == 4 and ahead:
                            average(sums, b * 2 + 3)
                    turn(DT - 2)
                    turn(DT - 1)

            both(pe, program)

        @block.scalar
        def _(act):
            act.sem_inc(turn_free, 2)
            act.sem_inc(stored[0], 16)
            act.sem_inc(stored[1], 16)

            def att_high(b):
                act.wait_ge(at_in, b * 16 + 16)
                nc.scalar.copy(ah[:, :, :], atf[:, :, :]).then_inc(a_high, 1)

            act.wait_ge(at_in, 16)
            nc.scalar.copy(ah[:, :, :], atf[:, :, :]).then_inc(a_high, 1)
            act.wait_ge(filled, DT)
            att_high(1)

            def program(it, final):
                for k in range(2):
                    b = it * 2 + k
                    ahead = not (final and k == 1)
                    act.wait_ge(centred, b + 1)
                    nc.scalar.activation(sq[:, :, :], cen[:, :, :], ACT.Square).then_inc(squared, 1)
                    act.wait_ge(averaged, b * 2 + 2)
                    nc.scalar.activation(rec[:, :], STATS[:, 0:TC], ACT.Sqrt, bias=LN_EPS).then_inc(rooted, 1)
                    act.wait_ge(scaled, b + 1)
                    nc.scalar.copy(xh[:, :, :], cen[:, :, :]).then_inc(x_high, 1)
                    act.wait_ge(diff, b + 1)
                    nc.scalar.activation(pw[:, 1, :], pw[:, 0, :], ACT.Exp).then_inc(expd, 1)
                    act.wait_ge(low_f, b + 1)
                    nc.scalar.copy(z[:, :], LOW[:, 0:TC]).then_inc(low_out, 1)
                    for pair in range(DT // 2):
                        if pair == 1 and not final:
                            att_high(b + 2)
                        act.wait_ge(turned, b * DT + 2 * pair + 4)
                        act.wait_ge(stored[pair % 2], (b * 2 + pair // 2) * 16 + 16)
                        nc.scalar.copy(ost[pair % 2][:, :, :], TURN[pair % 2][:, 0:512].rearrange("p (t o) -> p t o", t=TT))\
                            .then_inc(turn_free, 1)

            both(act, program)

        @block.gpsimd
        def _(pool):
            def att_low(b):
                pool.wait_ge(a_high, b + 1)
                nc.gpsimd.tensor_tensor(out=al[:, :, :], in0=atf[:, :, :], in1=ah[:, :, :].bitcast(F32),
                                        op=ALU.subtract).then_inc(a_low, 1)

            att_low(0)
            att_low(1)

            def program(it, final):
                for k in range(2):
                    b = it * 2 + k
                    pool.wait_ge(x_high, b + 1)
                    d = slice(DK // 2, DK)
                    nc.gpsimd.tensor_tensor(out=xl[:, d, :], in0=cen[:, d, :], in1=xh[:, d, :].bitcast(F32),
                                            op=ALU.subtract).then_inc(x_low_p, 1)
                    if not final:
                        att_low(b + 2)

            both(pool, program)

        @block.vector
        def _(dve):
            dve.sem_inc(freed, 2)

            def leave_projection(r, slot, ot, half_in):
                dve.wait_ge(filled, r + 1)
                if half_in is not None:
                    dve.wait_ge(h_in[ot // (DT // 2)], half_in)
                stt(hb[slot][:, ot, :], ACC[ot % 2][:, 0:TC], bo[:, ot:ot + 1], hb[slot][:, ot, :], ALU.add, ALU.add)\
                    .then_inc(freed, 1)

            def sum_features(source):
                return nc.vector.tensor_reduce(out=sums[:, :], in_=source[:, :, :].rearrange("p a t -> p t a"), axis=AX.X,
                                               op=ALU.add)

            for ot in range(DT):
                leave_projection(ot, 0, ot, 16 if ot % (DT // 2) == 0 else None)
            dve.wait_ge(freed, DT + 2)
            sum_features(hb[0]).then_inc(summed, 1)

            def program(it, final):
                for k in range(2):
                    b = it * 2 + k
                    ahead = not (final and k == 1)
                    r0 = b * (2 * DT) + DT
                    nxt = 1 - k

                    def project_out(ot):
                        if ahead:
                            leave_projection(r0 + ot, nxt, ot, (b + 1) * 16 + 16 if ot % (DT // 2) == 0 else None)

                    dve.wait_ge(averaged, b * 2 + 1)
                    if ahead:
                        dve.wait_ge(a_low, b + 2)
                    tt(cen[:, :, :], hb[k][:, :, :], spread(STATS[:, 0:TC], 1, DK), ALU.subtract).then_inc(centred, 1)
                    project_out(0)
                    dve.wait_ge(squared, b + 1)
                    sum_features(sq).then_inc(summed, 1)
                    project_out(1)
                    project_out(2)
                    dve.wait_ge(rooted, b + 1)
                    base = b * 5
                    nc.vector.reciprocal(rec[:, :], rec[:, :]).then_inc(nstep, 1)
                    dve.wait_ge(nstep, base + 1)
                    tt(nwt[:, :], rec[:, :], rec[:, :], ALU.mult).then_inc(nstep, 1)
                    dve.wait_ge(nstep, base + 2)
                    stt(nwt[:, :], STATS[:, 0:TC], LN_EPS, nwt[:, :], ALU.add, ALU.mult).then_inc(nstep, 1)
                    dve.wait_ge(nstep, base + 3)
                    ts(nwt[:, :], nwt[:, :], -0.5, 1.5, ALU.mult, ALU.add).then_inc(nstep, 1)
                    dve.wait_ge(nstep, base + 4)
                    tt(rec[:, :], rec[:, :], nwt[:, :], ALU.mult).then_inc(nstep, 1)
                    project_out(3)
                    dve.wait_ge(nstep, base + 5)
                    tt(cen[:, :, :], cen[:, :, :], spread(rec[:, :], 1, DK), ALU.mult).then_inc(scaled, 1)
                    project_out(4)
                    project_out(5)
                    dve.wait_ge(x_high, b + 1)
                    d = slice(0, DK // 2)
                    tt(xl[:, d, :], cen[:, d, :], xh[:, d, :].bitcast(F32), ALU.subtract).then_inc(x_low_d, 1)
                    project_out(6)
                    project_out(7)
                    if ahead:
                        r0 = r0 + DT
                        dve.wait_ge(freed, r0 + 2)
                        sum_features(hb[nxt]).then_inc(summed, 1)

                    steps = [0]

                    def link(ins):
                        steps[0] += 1
                        ins.then_inc(gstep, 1)
                        dve.wait_ge(gstep, b * GATE_STEPS + steps[0])

                    dve.wait_ge(gated, b + 1)
                    link(nc.vector.tensor_copy(lg[:, :, :], GATE[:, 0:TT * NE].rearrange("p (t e) -> p t e", e=NE)))
                    nc.vector.memset(fence[:, :], 0.0)
                    for t in range(TT):
                        ins = nc.vector.max(m8[:, t, :], lg[:, t, :])
                        if t == TT - 1:
                            link(ins)
                    tt(pw[:, 0, :], m8[:, :, 1], m8[:, :, 0], ALU.subtract).then_inc(diff, 1)
                    tt(cmp, spread(lg[:, :, :], 2, NE), spread(lg[:, :, :], 3, NE), ALU.is_gt)
                    link(tt(eq, spread(lg[:, :, :], 2, NE), spread(lg[:, :, :], 3, NE), ALU.is_equal))
                    link(tt(eq, eq, spread(tri[:, :, :], 1, TT), ALU.mult))
                    link(tt(cmp, cmp, eq, ALU.add))
                    link(nc.vector.tensor_reduce(out=rank[:, :], in_=cmp, axis=AX.X, op=ALU.add))
                    dve.wait_ge(expd, b + 1)
                    link(ts(pw[:, 2, :], pw[:, 1, :], 1.0, None, ALU.add))
                    link(nc.vector.reciprocal(pw[:, 2, :], pw[:, 2, :]))
                    link(tt(pw[:, 3, :], pw[:, 1, :], pw[:, 2, :], ALU.mult))
                    for q in range(2):
                        ins = stt(wsel[:, q, :, :], rank[:, :].rearrange("p (t e) -> p t e", e=NE), float(q),
                                  spread(pw[:, 2 + q, :], 2, NE), ALU.is_equal, ALU.mult)
                        link(ins)
                    link(ts(wsel[:, :, :, :], wsel[:, :, :, :], LORA_SCALE, None, ALU.mult))
                    tt(wx, spread(wsel[:, 0, :, :], 3, RANK), spread(wsel[:, 1, :, :], 3, RANK), ALU.add).then_inc(wx_ready, 1)
                    assert steps[0] == GATE_STEPS
                    dve.wait_ge(low_out, b + 1)
                    dve.wait_ge(wx_turned, b + 1)
                    tt(z[:, :], z[:, :], GATE[:, P:P + TC], ALU.mult).then_inc(z_ready, 1)
                    for ot in range(DT):
                        dve.wait_ge(filled, r0 + ot + 1)
                        dve.wait_ge(turned, b * DT + ot + 1)
                        stt(y[ot % 2][:, :], ACC[ot % 2][:, 0:TC], bb[:, ot:ot + 1], hb[k][:, ot, :], ALU.add, ALU.add)\
                            .then_inc(freed, 1)

            both(dve, program)


def program(nc, x, log_dt, b_ri, inv_a, a_imag, w_qkv, b_qkv, w_out, b_out, gate_w, base_w, base_b, lora_a, lora_b,
            out, h_dram, attn_dram):
    def sem(name):
        return nc.alloc_semaphore(name)

    psum = [nc.alloc_psum_tensor(f"bank{k}", [P, 512], F32) for k in range(8)]
    CR = Region(nc, "const_", CONST_AT, CONST_AT + CONST_BYTES)
    ident, mean_w = CR("ident", [P, P]), CR("mean_w", [P, P])
    H = nc.alloc_sbuf_tensor_at("h", [P, DK, BATCH, SEQ], F32, offset=H_AT)
    XH = nc.alloc_sbuf_tensor_at("x_high", [P, DK, TOK], F32R, offset=X_AT)
    XL = nc.alloc_sbuf_tensor_at("x_low", [P, DK, TOK], F32R, offset=X_AT + X_BYTES // 2)
    constants(nc, sem, ident, mean_w)
    s4d_stage(nc, sem, psum, x, log_dt, b_ri, inv_a, a_imag, ident, H)
    norm_stage(nc, sem, psum, mean_w, H, XH, XL, h_dram)
    attention_stage(nc, sem, psum, ident, XH, XL, w_qkv, b_qkv, attn_dram)
    output_stage(nc, sem, psum, ident, mean_w, h_dram, attn_dram, w_out, b_out, gate_w, base_w, base_b, lora_a, lora_b,
                 out.rearrange("b s o -> (b s) o"))


_INS = ["x", "L0_tok_log_dt", "L0_tok_B", "L0_tok_inv_A_real", "L0_tok_A_imag", "L0_attn_w_qkv", "L0_attn_b_qkv",
        "L0_attn_w_out", "L0_attn_b_out", "L0_ffn_gate_w", "L0_ffn_base_w", "L0_ffn_base_b", "L0_ffn_lora_A",
        "L0_ffn_lora_B"]


def kernel(**inputs):
    import concourse.bacc as _bacc
    from concourse.bass_utils import run_bass_kernel_spmd as _run

    nc = _bacc.Bacc("TRN2", target_bir_lowering=False, num_devices=1)
    arrays, args = {}, []
    for name in _INS:
        a = np.ascontiguousarray(inputs[name])
        arrays[f"in_{name}"] = a
        args.append(nc.dram_tensor(f"in_{name}", list(a.shape), mybir.dt.from_np(a.dtype), kind="ExternalInput").ap())
    args.append(nc.dram_tensor("out", [BATCH, SEQ, DM], F32, kind="ExternalOutput").ap())
    args.append(nc.dram_tensor("h_scratch", [NTC, P, DK, TC // SEQ, SEQ], F32, kind="Internal").ap())
    args.append(nc.dram_tensor("attended_scratch", [NG, P, TOK], F32, kind="Internal").ap())
    program(nc, *args)
    r = _run(nc, [arrays], core_ids=[0])
    return r.results[0]["out"]
```

```python
import concourse.bass as bass
from concourse import mybir
from concourse.alu_op_type import AluOpType as ALU
import numpy as np

F32 = mybir.dt.float32
F32R = mybir.dt.float32r
I32 = mybir.dt.int32
ACT = mybir.ActivationFunctionType
AX = mybir.AxisListType

P = 128
BATCH, SEQ, NSTATE = 16, 128, 64
DM = 1024
DK = DM // P
TOK = BATCH * SEQ
NHEAD, HD = 32, 32
HG = P // HD
NG = NHEAD // HG
TB = 512
NTB = TOK // TB
CB = TB // SEQ
NE, RANK = 8, 16
QK_SCALE = 1.0 / float(np.sqrt(HD))
LORA_SCALE = 32.0 / 16.0
LN_EPS = 1e-5

NA, NI, NJ = DM // P, 8, 16
NF = NA + NI + NJ
SU = 8

CONST_AT = 16512
CONST_BYTES = 1536
X_AT = CONST_AT + CONST_BYTES
X_BYTES = 2 * DK * TOK * 4
H_AT = X_AT + X_BYTES
H_BYTES = DK * TOK * 4
T_AT = H_AT + H_BYTES
MEAN_BYTES = TOK * 4
END_AT = 229368


class Region:

    def __init__(self, nc, tag, start, end):
        self.nc, self.tag, self.at, self.end = nc, tag, start, end

    def __call__(self, name, shape, dtype=F32):
        size = 4
        for n in shape[1:]:
            size *= n
        t = self.nc.alloc_sbuf_tensor_at(self.tag + name, list(shape), dtype, offset=self.at)
        self.at += (size + 31) // 32 * 32
        assert self.at <= self.end, (name, self.at, self.end)
        return t


def spread(ap, dim, n):
    shape = list(ap.shape)
    shape.insert(dim, n)
    return ap.unsqueeze(dim).broadcast_to(shape)


def constants(nc, sem, ident, mean_w):
    made = sem("constants_made")
    with nc.Block() as block:
        @block.gpsimd
        def _(pool):
            nc.gpsimd.memset(ident[:, :], 0.0).then_inc(made, 1)
            nc.gpsimd.memset(mean_w[:, :], 1.0 / DM)
            pool.wait_ge(made, 1)
            nc.gpsimd.affine_select(out=ident[:, :], in_=ident[:, :], compare_op=ALU.not_equal, fill=1.0,
                                    base=0, pattern=[[-1, P]], channel_multiplier=1)


def s4d_stage(nc, sem, psum, x, log_dt, b_ri, inv_a, a_imag, ident, mean_w, H, means):
    R = Region(nc, "s4_", X_AT, X_AT + X_BYTES)
    X1, X2, V1, V2, U1, U2, Y1, Y2 = 0, 16, 32, 48, 64, 72, 80, 88
    NT = 96
    FT = R("factorsT", [P, NT, SEQ])
    mark = R.at
    xr = R("x", [P, BATCH, NSTATE, 2])
    xs = R("x_im_re", [P, BATCH, NSTATE, 2])
    turns = R("turns", [P, 2, NF, NSTATE])
    near = R("near", [P, 2, NF, NSTATE])
    decay = R("decay", [P, NF, NSTATE])
    HR = Region(nc, "s4h_", H_AT, H_AT + H_BYTES)
    fac = HR("factors", [P, NF, NSTATE, 2])
    vv = HR("v", [P, 2, NJ, NSTATE, 2])
    u2 = HR("u2", [P, NI, NSTATE, 2])
    y1 = HR("y1", [P, NA, NSTATE, 2])
    y2 = HR("y2", [P, NA, NSTATE, 2])
    gt = HR("gt", [P, 2, NA, NSTATE])
    ea = HR("exp_in", [P, 2 * NSTATE + 1])
    em = [HR(f"em{k}", [P, 2 * NSTATE + 1]) for k in range(7)]
    emi = HR("emi", [P, 2 * NSTATE + 1], I32)
    bri = HR("b", [P, NSTATE, 2])
    aim = HR("a_imag", [P, NSTATE])
    c = [HR(f"c{k}", [P, NSTATE]) for k in range(24)]
    mi = HR("mult_i", [P, NF], I32)
    mf = HR("mult", [P, NF])

    loaded, iotas = sem("s4_loaded"), sem("s4_iotas")
    chain, trig, trig_in = sem("s4_chain"), sem("s4_trig"), sem("s4_trig_in")
    swapped, doubled, ready, tposed, evac = sem("s4_swapped"), sem("s4_doubled"), sem("s4_ready"), sem("s4_tposed"), [sem("s4_evacA"), sem("s4_evacD")]
    ROUND = 1.5 * 2.0 ** 23
    sig, th, u, ar, expm1 = c[0], c[1], c[2], c[3], c[4]

    with nc.Block() as block:
        @block.sync
        def _(sp):
            sp.dma_start(ea[:, 0:NSTATE], inv_a).then_inc(loaded, 16)
            sp.dma_start(ea[:, NSTATE:NSTATE + 1], log_dt.rearrange("(s o) -> s o", o=1)).then_inc(loaded, 16)
            sp.dma_start(aim[:, :], a_imag).then_inc(loaded, 16)
            sp.dma_start(bri[:, :, :], b_ri).then_inc(loaded, 16)
            sp.dma_start(xr[:, :, :, :], x.rearrange("b s n r -> s b n r")).then_inc(loaded, 16)

        @block.gpsimd
        def _(pool):
            nc.gpsimd.iota(mi[:, 0:NA], pattern=[[P, NA]], base=0, channel_multiplier=0).then_inc(iotas, 1)
            nc.gpsimd.iota(mi[:, NA:NA + NI], pattern=[[NJ, NI]], base=0, channel_multiplier=0).then_inc(iotas, 1)
            nc.gpsimd.iota(mi[:, NA + NI:NF], pattern=[[1, NJ]], base=0, channel_multiplier=0).then_inc(iotas, 1)

        @block.vector
        def _(dve):
            steps = [0]

            def link(ins):
                steps[0] += 1
                ins.then_inc(chain, 1)
                dve.wait_ge(chain, steps[0])

            tt, ts, stt = nc.vector.tensor_tensor, nc.vector.tensor_scalar, nc.vector.scalar_tensor_tensor

            def exact_exp(dst, dst_m1, src, n):
                v, k, r, p, s = (em[q][:, 0:n] for q in range(5))
                link(ts(v, src, -87.0, 88.0, ALU.max, ALU.min))
                link(ts(k, v, float(np.log2(np.e)), ROUND, ALU.mult, ALU.add))
                link(ts(k, k, ROUND, None, ALU.subtract))
                link(stt(r, k, -0.693145751953125, v, ALU.mult, ALU.add))
                link(stt(r, k, -1.42860682030941723e-6, r, ALU.mult, ALU.add))
                link(ts(p, r, 1.0 / 40320, None, ALU.mult))
                for q in (5040, 720, 120, 24, 6, 2, 1):
                    link(stt(p, p, 1.0 / q, r, ALU.add, ALU.mult))
                link(ts(emi[:, 0:n], k, 127.0, 2.0 ** 23, ALU.add, ALU.mult))
                two_k = emi[:, 0:n].bitcast(F32)
                link(ts(s, two_k, 1.0, None, ALU.subtract))
                link(tt(p, p, two_k, ALU.mult))
                link(tt(dst_m1, p, s, ALU.add))
                if dst is not None:
                    link(tt(dst, p, two_k, ALU.add))

            dve.wait_ge(iotas, 3)
            link(nc.vector.tensor_copy(mf[:, :], mi[:, :]))
            dve.wait_ge(loaded, 80)
            exact_exp(em[5][:, 0:NSTATE + 1], em[6][:, 0:NSTATE + 1], ea[:, 0:NSTATE + 1], NSTATE + 1)
            dt = em[5][:, NSTATE:NSTATE + 1]
            link(ts(ar[:, :], em[5][:, 0:NSTATE], -1.0, None, ALU.mult))
            link(ts(sig[:, :], ar[:, :], dt, None, ALU.mult))
            link(ts(th[:, :], aim[:, :], dt, None, ALU.mult))
            link(ts(c[5][:, :], th[:, :], 1.0 / (2 * np.pi), ROUND, ALU.mult, ALU.add))
            link(ts(c[5][:, :], c[5][:, :], ROUND, None, ALU.subtract))
            link(stt(c[6][:, :], c[5][:, :], -6.28125, th[:, :], ALU.mult, ALU.add))
            link(stt(c[6][:, :], c[5][:, :], -(2 * np.pi - 6.28125), c[6][:, :], ALU.mult, ALU.add))
            link(ts(u[:, :], c[6][:, :], 1.0 / (2 * np.pi), None, ALU.mult))
            link(tt(turns[:, 1, :, :], spread(u[:, :], 1, NF), spread(mf[:, :], 2, NSTATE), ALU.mult))
            link(ts(turns[:, 0, :, :], turns[:, 1, :, :], 0.25, None, ALU.add))
            link(ts(near[:, :, :, :], turns[:, :, :, :], ROUND, ROUND, ALU.add, ALU.subtract))
            link(tt(near[:, :, :, :], near[:, :, :, :], turns[:, :, :, :], ALU.subtract))
            link(ts(near[:, :, :, :], near[:, :, :, :], 0.4999999, -0.4999999, ALU.min, ALU.max))
            tt(decay[:, :, :], spread(sig[:, :], 1, NF), spread(mf[:, :], 2, NSTATE), ALU.mult).then_inc(trig_in, 1)
            exact_exp(None, expm1[:, :], sig[:, :], NSTATE)
            dve.wait_ge(trig, 4)
            half, sn = c[7], c[8]
            link(tt(c[9][:, :], half[:, :], half[:, :], ALU.mult))
            link(ts(c[9][:, :], c[9][:, :], -2.0, None, ALU.mult))
            link(ts(c[10][:, :], expm1[:, :], 1.0, None, ALU.add))
            link(tt(c[11][:, :], c[10][:, :], c[9][:, :], ALU.mult))
            link(tt(c[11][:, :], c[11][:, :], expm1[:, :], ALU.add))
            link(tt(c[12][:, :], c[10][:, :], sn[:, :], ALU.mult))
            link(tt(c[13][:, :], ar[:, :], ar[:, :], ALU.mult))
            link(tt(c[14][:, :], aim[:, :], aim[:, :], ALU.mult))
            link(tt(c[13][:, :], c[13][:, :], c[14][:, :], ALU.add))
            link(nc.vector.reciprocal(c[14][:, :], c[13][:, :]))
            link(tt(c[15][:, :], c[11][:, :], ar[:, :], ALU.mult))
            link(tt(c[16][:, :], c[12][:, :], aim[:, :], ALU.mult))
            link(tt(c[15][:, :], c[15][:, :], c[16][:, :], ALU.add))
            link(tt(c[15][:, :], c[15][:, :], c[14][:, :], ALU.mult))
            link(tt(c[16][:, :], c[12][:, :], ar[:, :], ALU.mult))
            link(tt(c[17][:, :], c[11][:, :], aim[:, :], ALU.mult))
            link(tt(c[16][:, :], c[16][:, :], c[17][:, :], ALU.subtract))
            link(tt(c[16][:, :], c[16][:, :], c[14][:, :], ALU.mult))
            link(ts(c[18][:, :], bri[:, :, 0], 2.0, None, ALU.mult))
            link(ts(c[19][:, :], bri[:, :, 1], 2.0, None, ALU.mult))
            link(tt(c[20][:, :], c[15][:, :], c[18][:, :], ALU.mult))
            link(tt(c[21][:, :], c[16][:, :], c[19][:, :], ALU.mult))
            link(tt(c[20][:, :], c[20][:, :], c[21][:, :], ALU.subtract))
            link(tt(c[21][:, :], c[15][:, :], c[19][:, :], ALU.mult))
            link(tt(c[22][:, :], c[16][:, :], c[18][:, :], ALU.mult))
            link(tt(c[21][:, :], c[21][:, :], c[22][:, :], ALU.add))
            gr, gi = c[20], c[21]
            tt(fac[:, :, :, 0], decay[:, :, :], near[:, 0, :, :], ALU.mult)
            link(tt(fac[:, :, :, 1], decay[:, :, :], near[:, 1, :, :], ALU.mult))
            ts(u2[:, :, :, 0], fac[:, NA:NA + NI, :, 1], -1.0, None, ALU.mult)
            nc.vector.tensor_copy(u2[:, :, :, 1], fac[:, NA:NA + NI, :, 0]).then_inc(ready, 1)
            pr, pi = fac[:, 0:NA, :, 0], fac[:, 0:NA, :, 1]
            GR, GI = spread(gr[:, :], 1, NA), spread(gi[:, :], 1, NA)
            tt(gt[:, 0, :, :], GR, pr, ALU.mult)
            link(tt(gt[:, 1, :, :], GI, pi, ALU.mult))
            link(tt(y1[:, :, :, 0], gt[:, 0, :, :], gt[:, 1, :, :], ALU.subtract))
            ts(y1[:, :, :, 1], y1[:, :, :, 0], -1.0, None, ALU.mult)
            tt(gt[:, 0, :, :], GR, pi, ALU.mult)
            link(tt(gt[:, 1, :, :], GI, pr, ALU.mult))
            link(stt(y2[:, :, :, 0], gt[:, 0, :, :], -1.0, gt[:, 1, :, :], ALU.mult, ALU.subtract))
            nc.vector.tensor_copy(y2[:, :, :, 1], y2[:, :, :, 0]).then_inc(ready, 1)
            for g in range(1, NT // 4, 2):
                dve.wait_ge(tposed, g + 1)
                nc.vector.tensor_copy(FT[:, 4 * g:4 * g + 4, :], psum[g % 8][:, 0:512]).then_inc(evac[1], 1)

        @block.scalar
        def _(act):
            act.wait_ge(loaded, 80)
            nc.scalar.copy(xs[:, :, :, 0], xr[:, :, :, 1])
            nc.scalar.copy(xs[:, :, :, 1], xr[:, :, :, 0]).then_inc(swapped, 1)
            act.wait_ge(trig_in, 1)
            nc.scalar.activation(near[:, :, :, :], near[:, :, :, :], ACT.Sin, scale=-2 * np.pi).then_inc(trig, 1)
            nc.scalar.activation(c[7][:, :], u[:, :], ACT.Sin, scale=np.pi).then_inc(trig, 1)
            nc.scalar.activation(c[8][:, :], u[:, :], ACT.Sin, scale=6.283185).then_inc(trig, 1)
            nc.scalar.activation(decay[:, :, :], decay[:, :, :], ACT.Exp).then_inc(trig, 1)
            act.wait_ge(ready, 1)
            for part in range(2):
                ins = nc.scalar.copy(vv[:, part, :, :, :], spread(fac[:, NA + NI:NF, :, part], 3, 2))
            ins.then_inc(doubled, 1)
            for g in range(0, NT // 4, 2):
                act.wait_ge(tposed, g + 1)
                nc.scalar.copy(FT[:, 4 * g:4 * g + 4, :], psum[g % 8][:, 0:512]).then_inc(evac[0], 1)

        @block.tensor
        def _(pe):
            def source(t):
                if t < X2:
                    return xr[:, t, :, :]
                if t < V1:
                    return xs[:, t - X2, :, :]
                if t < U1:
                    return vv[:, (t - V1) // NJ, (t - V1) % NJ, :, :]
                if t < U2:
                    return fac[:, NA + t - U1, :, :]
                if t < Y1:
                    return u2[:, t - U2, :, :]
                if t < Y2:
                    return y1[:, t - Y1, :, :]
                return y2[:, t - Y2, :, :]

            pe.wait_ge(swapped, 1)
            for g in range(NT // 4):
                if 4 * g == V1:
                    pe.wait_ge(doubled, 1)
                if 4 * g == Y1:
                    pe.wait_ge(ready, 2)
                if g >= 8:
                    pe.wait_ge(evac[g % 2], (g - 8) // 2 + 1)
                for t in range(4 * g, 4 * g + 4):
                    ins = nc.tensor.transpose(psum[g % 8][:, (t % 4) * P:(t % 4 + 1) * P], source(t), ident[:, :])
                ins.then_inc(tposed, 1)

    R2 = Region(nc, "s4u_", mark, X_AT + X_BYTES)
    q12 = [R2(f"q12_{k}", [P, 2, SU, P]) for k in range(2)]
    w12 = [R2(f"w12_{k}", [P, 2, SU, BATCH * NA]) for k in range(2)]
    qf = [R2(f"q_{k}", [P, SU, P]) for k in range(2)]
    wf = [R2(f"w_{k}", [P, SU, BATCH * NA]) for k in range(2)]
    parts_w, parts_q, w12_free = sem("s4_parts_w"), sem("s4_parts_q"), sem("s4_w12_free")
    sums, filled, freed = sem("s4_sums"), sem("s4_filled"), sem("s4_freed")
    averaged, mean_out = sem("s4_averaged"), sem("s4_mean_out")
    UNITS = SEQ // SU
    tt = nc.vector.tensor_tensor

    with nc.Block() as block:
        @block.gpsimd
        def _(pool):
            with pool.Fori(0, UNITS // 2) as it:
                for k in range(2):
                    at = bass.ds(it * (2 * SU) + k * SU, SU)
                    pool.wait_ge(w12_free, it * 2 + k + 1)
                    for part, (fx, fy) in enumerate(((X1, Y1), (X2, Y2))):
                        ins = nc.gpsimd.tensor_tensor(
                            out=w12[k][:, part, :, :].rearrange("p s (c a) -> p s c a", a=NA),
                            in0=spread(FT[:, fx:fx + BATCH, at].rearrange("p c s -> p s c"), 3, NA),
                            in1=spread(FT[:, fy:fy + NA, at].rearrange("p a s -> p s a"), 2, BATCH), op=ALU.mult)
                    ins.then_inc(parts_w, 1)

        @block.vector
        def _(dve):
            dve.sem_inc(w12_free, 2)
            with dve.Fori(0, UNITS // 2) as it:
                for k in range(2):
                    at = bass.ds(it * (2 * SU) + k * SU, SU)
                    for part, (fu, fv) in enumerate(((U1, V1), (U2, V2))):
                        ins = tt(q12[k][:, part, :, :].rearrange("p s (i j) -> p s i j", j=NJ),
                                 spread(FT[:, fu:fu + NI, at].rearrange("p i s -> p s i"), 3, NJ),
                                 spread(FT[:, fv:fv + NJ, at].rearrange("p j s -> p s j"), 2, NI), ALU.mult)
                    ins.then_inc(parts_q, 1)
                    dve.wait_ge(freed, it * 2 + k + 1)
                    dve.wait_ge(parts_w, it * 2 + k + 1)
                    tt(wf[k][:, :, :], w12[k][:, 0, :, :], w12[k][:, 1, :, :], ALU.add).then_inc(w12_free, 1)
                    dve.wait_ge(parts_q, it * 2 + k + 1)
                    tt(qf[k][:, :, :], q12[k][:, 0, :, :], q12[k][:, 1, :, :], ALU.add).then_inc(sums, 1)

        @block.tensor
        def _(pe):
            with pe.Fori(0, UNITS // 2) as it:
                for k in range(2):
                    pe.wait_ge(sums, it * 2 + k + 1)
                    pe.wait_ge(freed, it * 2 + k + 1)
                    for s in range(SU):
                        ins = nc.tensor.matmul(psum[2 * k + s // 4][:, (s % 4) * P:(s % 4 + 1) * P],
                                               qf[k][:, s, :], wf[k][:, s, :], start=True, stop=True)
                        if s == 3:
                            ins.then_inc(filled, 1)
                    ins.then_inc(filled, 1)
                pe.wait_ge(freed, it * 2 + 4)
                pe.wait_ge(mean_out, it + 1)
                for a in range(DK):
                    ins = nc.tensor.matmul(psum[4][:, 0:BATCH * 2 * SU], mean_w[:, :], H[:, a, :, bass.ds(it * (2 * SU), 2 * SU)],
                                           start=(a == 0), stop=(a == DK - 1))
                ins.then_inc(averaged, 1)

        @block.scalar
        def _(act):
            act.sem_inc(freed, 2)
            act.sem_inc(mean_out, 1)
            with act.Fori(0, UNITS // 2) as it:
                for k in range(2):
                    for half in range(2):
                        act.wait_ge(filled, it * 4 + 2 * k + half + 1)
                        ins = nc.scalar.copy(
                            H[:, :, :, bass.ds(it * (2 * SU) + k * SU + 4 * half, 4)].rearrange("p a c s -> p s c a"),
                            psum[2 * k + half][:, 0:512].rearrange("p (s c a) -> p s c a", s=4, a=NA))
                    ins.then_inc(freed, 1)
                act.wait_ge(averaged, it + 1)
                nc.scalar.activation(means[:, :, bass.ds(it * (2 * SU), 2 * SU)],
                                     psum[4][:, 0:BATCH * 2 * SU].rearrange("p (c s) -> p c s", c=BATCH), ACT.Copy)\
                    .then_inc(mean_out, 1)


LB = 4


def norm_stage(nc, sem, psum, ident, mean_w, H, means, XH, XL, wh, wl, w_qkv, h_dram):
    T = Region(nc, "ln_", T_AT + MEAN_BYTES, END_AT)
    cen = nc.alloc_sbuf_tensor_at("ln_centred", [P, DK, TOK], F32, offset=X_AT + X_BYTES // 2)
    sq = nc.alloc_sbuf_tensor_at("ln_squares", [P, DK, TOK], F32, offset=X_AT)
    var = psum[0]
    log_var, rec, nwt = T("log_var", [P, LB * SEQ]), T("reciprocal", [P, LB * SEQ]), T("newton", [P, LB * SEQ])
    w_raw = [nc.alloc_sbuf_tensor_at(f"ln_w_raw{j}", [P, DM], F32, offset=H_AT + (2 * 2 * 3 + j) * DM * 4) for j in range(3)]
    w_in, w_turned, w_high, w_low = [sem(f"ln_w_in{j}") for j in range(3)], sem("ln_w_turned"), sem("ln_w_high"), sem("ln_w_low")
    HALVES = [(j, slice(0, DK // 2)) if q == 0 else (j, slice(DK // 2, DK)) for j in range(3) for q in range(2)]
    stored, centred, squared, averaged = sem("ln_stored"), sem("ln_centred"), sem("ln_squared"), sem("ln_averaged")
    logged, guessed, newton, scaled = sem("ln_logged"), sem("ln_guessed"), sem("ln_newton"), sem("ln_scaled")
    high, low = sem("ln_high"), sem("ln_low")
    tt, stt = nc.vector.tensor_tensor, nc.vector.scalar_tensor_tensor
    GROUPS = BATCH // LB

    def both(eng, program):
        with eng.Fori(0, GROUPS - 1) as g:
            program(g, False)
        program(GROUPS - 1, True)

    def of_batch(x, i):
        return x[:, :, bass.ds(i * SEQ, SEQ)]

    with nc.Block() as block:
        @block.sync
        def _(sp):
            for b in range(h_dram.shape[0]):
                sp.dma_start(h_dram[b], H[:, :, 2 * b:2 * b + 2, :]).then_inc(stored, 16)
            sp.wait_ge(stored, 16 * h_dram.shape[0])
            sp.wait_ge(centred, BATCH)
            for j in range(3):
                sp.dma_start(w_raw[j][:, :], w_qkv[j * DM:j * DM + P, :]).then_inc(w_in[j], 16)

        @block.vector
        def _(dve):
            def centre(i):
                tt(of_batch(cen, i), H[:, :, bass.ds(i, 1), :].rearrange("p a o s -> p a (o s)"),
                   spread(means[:, bass.ds(i, 1), :].rearrange("p o s -> p (o s)"), 1, DK), ALU.subtract).then_inc(centred, 1)

            def program(g, final):
                if not final:
                    for k in range(LB):
                        centre(g * LB + (LB + k))
                dve.wait_ge(guessed, g + 1)
                stt(nwt[:, :], rec[:, :], -0.5, rec[:, :], ALU.mult, ALU.mult).then_inc(newton, 1)
                dve.wait_ge(newton, g * 3 + 1)
                stt(nwt[:, :], var[:, :], LN_EPS, nwt[:, :], ALU.add, ALU.mult).then_inc(newton, 1)
                dve.wait_ge(newton, g * 3 + 2)
                stt(rec[:, :], nwt[:, :], 1.5, rec[:, :], ALU.add, ALU.mult).then_inc(newton, 1)
                dve.wait_ge(newton, g * 3 + 3)
                for k in range(LB):
                    i = g * LB + k
                    tt(of_batch(cen, i), of_batch(cen, i), spread(rec[:, k * SEQ:(k + 1) * SEQ], 1, DK), ALU.mult)\
                        .then_inc(scaled, 1)

            for k in range(LB):
                centre(k)
            both(dve, program)
            for n, (j, d) in enumerate(HALVES):
                dve.wait_ge(w_high, n + 1)
                tt(wl[:, j, d, :], psum[1 + n][:, :].rearrange("p (d o) -> p d o", o=P), wh[:, j, d, :].bitcast(F32),
                   ALU.subtract).then_inc(w_low, 1)

        @block.tensor
        def _(pe):
            def program(g, final):
                if final:
                    for n, (j, d) in enumerate(HALVES):
                        pe.wait_ge(w_in[j], 16)
                        for q in range(DK // 2):
                            ins = nc.tensor.transpose(psum[1 + n][:, q * P:(q + 1) * P],
                                                      w_raw[j][:, (d.start + q) * P:(d.start + q + 1) * P], ident[:, :])
                        ins.then_inc(w_turned, 1)
                for k in range(LB):
                    i = g * LB + k
                    pe.wait_ge(squared, i + 1)
                    for d in range(DK):
                        ins = nc.tensor.matmul(var[:, k * SEQ:(k + 1) * SEQ], mean_w[:, :], of_batch(sq, i)[:, d, :],
                                               start=(d == 0), stop=(d == DK - 1))
                ins.then_inc(averaged, 1)

            both(pe, program)

        @block.scalar
        def _(act):
            def square(i):
                act.wait_ge(centred, i + 1)
                nc.scalar.activation(of_batch(sq, i), of_batch(cen, i), ACT.Square).then_inc(squared, 1)

            def program(g, final):
                act.wait_ge(averaged, g + 1)
                nc.scalar.activation(log_var[:, :], var[:, :], ACT.Ln, bias=LN_EPS).then_inc(logged, 1)
                act.wait_ge(logged, g + 1)
                nc.scalar.activation(rec[:, :], log_var[:, :], ACT.Exp, scale=-0.5).then_inc(guessed, 1)
                act.wait_ge(newton, g * 3 + 2)
                if not final:
                    for k in range(LB):
                        square(g * LB + (LB + k))
                else:
                    for n, (j, d) in enumerate(HALVES):
                        act.wait_ge(w_turned, n + 1)
                        nc.scalar.copy(wh[:, j, d, :], psum[1 + n][:, :]).then_inc(w_high, 1)
                for k in range(LB):
                    i = g * LB + k
                    act.wait_ge(scaled, i + 1)
                    nc.scalar.copy(of_batch(XH, i), of_batch(cen, i)).then_inc(high, 1)

            for k in range(LB):
                square(k)
            both(act, program)

        @block.gpsimd
        def _(pool):
            with pool.Fori(0, GROUPS) as g:
                for k in range(LB):
                    i = g * LB + k
                    pool.wait_ge(high, i + 1)
                    nc.gpsimd.tensor_tensor(out=of_batch(XL, i), in0=of_batch(cen, i),
                                            in1=of_batch(XH, i).bitcast(F32), op=ALU.subtract).then_inc(low, 1)


Q, V, WA, WB, K, VT = "q", "v", "w first half", "w second half", "k", "v natural"
BANK_OF = {Q: 0, V: 1, WA: 1, WB: 1, K: 0, VT: 1}


class Items:

    def __init__(self):
        self.at, self.n, self.bank_n = {}, 0, [0, 0]

    def add(self, key, kind):
        b = BANK_OF[kind]
        self.at[key, kind] = (self.n, b, self.bank_n[b])
        self.n += 1
        self.bank_n[b] += 1


def attention_stage(nc, sem, psum, ident, XH, XL, wh, wl, w_qkv, b_qkv, attn_dram):
    R = Region(nc, "at_", H_AT + 4 * 3 * DM * 4, END_AT)
    wraw = R("w_raw", [P, DM])
    qT = [R(f"qT{k}", [P, TB]) for k in range(2)]
    kT = [R(f"kT{k}", [P, TB]) for k in range(2)]
    vT = R("vT", [P, TB])
    v1 = R("v_and_one", [P, CB, HG, HD + 1])
    sc = [R(f"scores{k}", [P, HG, SEQ]) for k in range(2)]
    pt = [R(f"probsT{k}", [P, HG, SEQ]) for k in range(2)]
    nbias = R("minus_alibi", [P, HG, SEQ])
    on = R("attended", [P, CB, HG, HD])
    ato = R("attendedT", [P, TB])
    mn = R("minima", [P, 2, HG])
    ri = R("inverse_sums", [P, 2, HG])
    bq = R("biases", [P, NG, 3])
    bg = R("group_biases", [P, 2, 3])
    fence = R("fence", [P, 1])
    S_BANKS, ACC, PT_BANK, PV_BANK = psum[0:4], psum[4:6], psum[6], psum[7]
    tt, ts = nc.vector.tensor_tensor, nc.vector.tensor_scalar
    iot = ato[:, 0:SEQ].bitcast(I32)

    pro, body, last = Items(), Items(), Items()
    for kind in (Q, V, K, VT):
        pro.add(0, kind)
    for its, final in ((body, False), (last, True)):
        for k in range(8):
            ahead = not (final and k == 7)
            wts = k % 4 < 3 and not (final and k >= 4)
            for kind in [Q, V] * ahead + [WA, WB] * wts + [K, VT] * ahead:
                its.add(k, kind)
    ITER = NG // 2

    filled = sem("at_acc_filled")
    freed = [sem("at_acc_freed0"), sem("at_acc_freed1")]
    w_loaded, w_high, b_loaded, bias_set, bias_ready = sem("at_w_loaded"), sem("at_w_high"), sem("at_b_loaded"), sem("at_bias_set"), sem("at_bias_ready")
    s_filled, scored, exped, t_filled = sem("at_s_filled"), sem("at_scored"), sem("at_exped"), sem("at_t_filled")
    at_filled, at_left, pt_ready, pv_filled, on_ready, inverted = sem("at_at_filled"), sem("at_at_left"), sem("at_pt_ready"), sem("at_pv_filled"), sem("at_on_ready"), sem("at_inverted")
    stored, halved = sem("at_stored"), sem("at_halved")

    def item(it, key, kind):
        if it is None:
            n, b, r = pro.at[key, kind]
            return b, n, r
        n, b, r = (last if isinstance(it, int) else body).at[key, kind]
        return b, it * body.n + (pro.n + n), it * body.bank_n[b] + (pro.bank_n[b] + r)

    def its_before(it, k):
        its = last if isinstance(it, int) else body
        here = [sum(1 for (key, _), (_, b, _) in its.at.items() if b == bank and key < k) for bank in range(2)]
        return [it * body.bank_n[b] + (pro.bank_n[b] + here[b]) for b in range(2)]

    def wait_filled(eng, it, key, kind):
        eng.wait_ge(filled, item(it, key, kind)[1] + 1)

    def wait_freed(eng, it, key, kind):
        b, _, r = item(it, key, kind)
        eng.wait_ge(freed[b], r + 2)

    def wait_bank(eng, it, key, kind):
        b, _, r = item(it, key, kind)
        eng.wait_ge(freed[b], r + 1)

    def bank_of(kind):
        return ACC[BANK_OF[kind]]

    def both(eng, program):
        with eng.Fori(0, ITER - 1) as it:
            program(it)
        program(ITER - 1)

    def weights_ahead(it, k):
        return not (isinstance(it, int) and k >= 4)

    def step_ahead(it, k):
        return not (isinstance(it, int) and k == 7)

    with nc.Block() as block:
        @block.sync
        def _(sp):
            def load(rows):
                sp.dma_start(wraw[:, :], w_qkv[rows, :]).then_inc(w_loaded, 16)

            with nc.allow_non_contiguous_dma("a bias a feature"):
                for j in range(3):
                    sp.dma_start(bq[:, :, j], b_qkv[j * DM:(j + 1) * DM].rearrange("(g p) -> p g", p=P)).then_inc(b_loaded, 16)
            load(slice(P, 2 * P))

            def program(it):
                for k in range(8):
                    g, tb = it * 2 + k // 4, k % 4
                    if tb < 3 and weights_ahead(it, k):
                        wait_filled(sp, it, k, WB)
                        j, gn = (tb + 1, g + 1) if tb < 2 else (0, g + 2)
                        if tb < 2 or weights_ahead(it, k + 4):
                            load(bass.ds(gn * P + j * DM, P))
                    sp.wait_ge(at_left, it * 8 + k + 2)
                    sp.dma_start(attn_dram[bass.ds(g, 1), :, tb * TB:(tb + 1) * TB].rearrange("o p t -> (o p) t"),
                                 ato[:, :]).then_inc(stored, 16)

            both(sp, program)
            sp.wait_ge(stored, 16 * (NG * NTB + 1))

        @block.gpsimd
        def _(pool):
            nc.gpsimd.iota(iot, pattern=[[1, SEQ]], base=1 - SEQ, channel_multiplier=0).then_inc(bias_set, 1)
            pool.wait_ge(bias_set, 2)
            nc.gpsimd.affine_select(out=nbias[:, :, :], in_=nbias[:, :, :], compare_op=ALU.is_ge, fill=1e30,
                                    base=0, pattern=[[0, HG], [-1, SEQ]], channel_multiplier=1).then_inc(bias_set, 1)

        @block.tensor
        def _(pe):
            def weight_transposes(it, key, kind, tile):
                first = 0 if kind == WA else DK // 2
                wait_bank(pe, it, key, kind)
                pe.wait_ge(w_loaded, tile * 16 + 16)
                for d in range(DK // 2):
                    ins = nc.tensor.transpose(bank_of(kind)[:, d * P:(d + 1) * P],
                                              wraw[:, (first + d) * P:(first + d + 1) * P], ident[:, :])
                ins.then_inc(filled, 1)

            def project(it, key, kind, par, tb, a, b):
                j = {Q: 0, K: 1, V: 2}[kind]
                if a == 0:
                    wait_bank(pe, it, key, kind)
                at = slice(tb * TB, (tb + 1) * TB)
                for m in range(a, b):
                    d, part = m // 3, m % 3
                    w, x = ((wl, XH), (wh, XL), (wh, XH))[part]
                    ins = nc.tensor.matmul(bank_of(kind)[:, :], w[par][:, j, d, :], x[:, d, at],
                                           start=(m == 0), stop=(m == 3 * DK - 1))
                if b == 3 * DK:
                    ins.then_inc(filled, 1)

            def v_natural(it, key):
                wait_bank(pe, it, key, VT)
                for c in range(CB):
                    ins = nc.tensor.transpose(bank_of(VT)[:, c * P:(c + 1) * P], vT[:, c * P:(c + 1) * P], ident[:, :])
                ins.then_inc(filled, 1)

            for kind in (Q, V, K):
                project(None, 0, kind, 0, 0, 0, 3 * DK)
            v_natural(None, 0)

            def program(it):
                for k in range(8):
                    g, tb, n = it * 2 + k // 4, k % 4, it * 8 + k
                    ahead, weights = step_ahead(it, k), tb < 3 and weights_ahead(it, k)
                    par_n, tb_n = (k + 1) // 4 % 2, (k + 1) % 4
                    q, kk = qT[k % 2], kT[k % 2]

                    def proj(kind, a, b):
                        if ahead:
                            project(it, k, kind, par_n, tb_n, a, b)

                    def transposes(c):
                        if c == 0:
                            pe.wait_ge(at_left, n + 1)
                        pe.wait_ge(exped, n * 4 + c + 1)
                        pe.wait_ge(pt_ready, n * 4 + c + 1)
                        for h in range(HG):
                            ins = nc.tensor.transpose(PT_BANK[:, h * P:(h + 1) * P], sc[c % 2][:, h, :], ident[:, :])
                        ins.then_inc(t_filled, 1)

                    def weigh(c):
                        pe.wait_ge(pt_ready, n * 4 + c + 2)
                        pe.wait_ge(on_ready, n * 4 + c + 1)
                        for h in range(HG):
                            ins = nc.tensor.matmul(PV_BANK[:, h * (HD + 1):(h + 1) * (HD + 1)], pt[c % 2][:, h, :],
                                                   v1[:, c, h, :], start=True, stop=True)
                        ins.then_inc(pv_filled, 1)

                    pe.wait_ge(scored, n * 4 + 4)
                    done = its_before(it, k)
                    pe.wait_ge(freed[0], done[0] + 1)
                    if ahead and tb == 3:
                        wait_freed(pe, it, k - 1, WB)
                    for c in range(CB):
                        for h in range(HG):
                            rows = slice(h * HD, (h + 1) * HD)
                            ins = nc.tensor.matmul(S_BANKS[h][:, c * P:(c + 1) * P], q[rows, c * P:(c + 1) * P],
                                                   kk[rows, c * P:(c + 1) * P], start=True, stop=True)
                        if c == CB - 1:
                            ins.then_inc(s_filled, 1)
                        proj(Q, 6 * c, 6 * c + 6)
                    proj(V, 0, 6)
                    pe.wait_ge(freed[1], done[1] + 1)
                    transposes(0)
                    proj(V, 6, 11)
                    weigh(0)
                    proj(V, 11, 16)
                    transposes(1)
                    proj(V, 16, 21)
                    weigh(1)
                    proj(V, 21, 24)
                    proj(K, 0, 2)
                    transposes(2)
                    proj(K, 2, 4)
                    if weights:
                        weight_transposes(it, k, WA, g * 3 + tb)
                    proj(K, 4, 7)
                    weigh(2)
                    proj(K, 7, 12)
                    if weights:
                        weight_transposes(it, k, WB, g * 3 + tb)
                    transposes(3)
                    proj(K, 12, 17)
                    weigh(3)
                    proj(K, 17, 24)
                    if ahead:
                        v_natural(it, k)
                    pe.wait_ge(on_ready, n * 4 + 5)
                    for c in range(CB):
                        ins = nc.tensor.transpose(PT_BANK[:, c * P:(c + 1) * P],
                                                  on[:, c, :, :].rearrange("p h d -> p (h d)"), ident[:, :])
                    ins.then_inc(at_filled, 1)

            both(pe, program)

        @block.scalar
        def _(act):
            act.sem_inc(stored, 16)
            act.sem_inc(at_left, 1)

            def leave_q(it, key, slot, par):
                wait_filled(act, it, key, Q)
                nc.scalar.activation(qT[slot][:, :], bank_of(Q)[:, :], ACT.Identity, scale=-QK_SCALE,
                                     bias=bg[:, par, 0:1]).then_inc(freed[0], 1)

            def leave_v(it, key, par):
                wait_filled(act, it, key, V)
                nc.scalar.activation(vT[:, :], bank_of(V)[:, :], ACT.Identity, bias=bg[:, par, 2:3]).then_inc(freed[1], 1)

            def leave_k(it, key, slot, par):
                wait_filled(act, it, key, K)
                nc.scalar.activation(kT[slot][:, :], bank_of(K)[:, :], ACT.Identity, bias=bg[:, par, 1:2]).then_inc(freed[0], 1)

            def weights_high(it, key, kind, par, j):
                first = 0 if kind == WA else DK // 2
                wait_filled(act, it, key, kind)
                nc.scalar.copy(wh[par][:, j, first:first + DK // 2, :], bank_of(kind)[:, :]).then_inc(w_high, 1)

            act.sem_inc(freed[0], 1)
            act.sem_inc(freed[1], 1)
            act.wait_ge(b_loaded, 48)
            nc.scalar.activation(bq[:, :, 0], bq[:, :, 0], ACT.Copy, scale=-QK_SCALE).then_inc(bias_ready, 1)
            act.wait_ge(bias_ready, 1)
            nc.scalar.copy(bg[:, 0, :], bq[:, 0, :]).then_inc(bias_ready, 1)
            act.wait_ge(bias_ready, 2)
            leave_q(None, 0, 0, 0)
            leave_v(None, 0, 0)
            leave_k(None, 0, 0, 0)

            def program(it):
                for k in range(8):
                    g, tb, n = it * 2 + k // 4, k % 4, it * 8 + k
                    ahead, weights = step_ahead(it, k), tb < 3 and weights_ahead(it, k)
                    par_n = (k // 4 + 1) % 2

                    def exps(c):
                        act.wait_ge(scored, n * 4 + c + 5)
                        for h in range(HG):
                            ins = nc.scalar.activation(sc[c % 2][:, h, :], sc[c % 2][:, h, :], ACT.Exp, scale=-1.0,
                                                       bias=mn[:, c % 2, h:h + 1])
                        ins.then_inc(exped, 1)

                    if ahead and tb == 3:
                        nc.scalar.copy(bg[:, par_n, :], bq[:, bass.ds(g + 1, 1), :].rearrange("p o j -> p (o j)")).then_inc(bias_ready, 1)
                    exps(0)
                    exps(1)
                    if ahead and tb == 3:
                        act.wait_ge(bias_ready, g + 3)
                    if ahead:
                        leave_q(it, k, (k + 1) % 2, (k + 1) // 4 % 2)
                    exps(2)
                    if ahead:
                        leave_v(it, k, (k + 1) // 4 % 2)
                    if weights:
                        weights_high(it, k, WA, par_n, tb)
                    exps(3)
                    if weights:
                        weights_high(it, k, WB, par_n, tb)
                    if ahead:
                        leave_k(it, k, (k + 1) % 2, (k + 1) // 4 % 2)
                    act.wait_ge(at_filled, n + 1)
                    act.wait_ge(stored, n * 16 + 16)
                    nc.scalar.copy(ato[:, :], PT_BANK[:, :]).then_inc(at_left, 1)

            both(act, program)

        @block.vector
        def _(dve):
            def weights_low(it, key, kind, par, j, tile):
                first = 0 if kind == WA else DK // 2
                dve.wait_ge(w_high, tile * 2 + (1 if kind == WA else 2))
                tt(wl[par][:, j, first:first + DK // 2, :], bank_of(kind)[:, :].rearrange("p (d o) -> p d o", o=P),
                   wh[par][:, j, first:first + DK // 2, :].bitcast(F32), ALU.subtract).then_inc(freed[BANK_OF[kind]], 1)

            def leave_v_natural(it, key):
                wait_filled(dve, it, key, VT)
                nc.vector.tensor_copy(v1[:, :, :, 0:HD], bank_of(VT)[:, :].rearrange("p (c h d) -> p c h d", c=CB, h=HG))\
                    .then_inc(freed[1], 1)

            dve.sem_inc(scored, 4)
            dve.sem_inc(pt_ready, 1)
            dve.sem_inc(on_ready, 1)
            nc.vector.memset(v1[:, :, :, HD:HD + 1], 1.0)
            dve.wait_ge(bias_set, 1)
            for h in range(HG):
                slope = float(np.float32(1.0) / np.float32(2.0) ** np.float32((h + 1) * 8.0 / NHEAD))
                ins = ts(nbias[:, h, :], iot, -2.0 * slope, None, ALU.mult)
            ins.then_inc(bias_set, 1)
            leave_v_natural(None, 0)
            dve.wait_ge(bias_set, 3)

            def program(it):
                for k in range(8):
                    g, tb, n = it * 2 + k // 4, k % 4, it * 8 + k
                    ahead, weights = step_ahead(it, k), tb < 3 and weights_ahead(it, k)
                    par_n = (k // 4 + 1) % 2

                    def score(c):
                        for h in range(HG):
                            ins = nc.vector.tensor_tensor_reduce(
                                out=sc[c % 2][:, h, :], in0=S_BANKS[h][:, c * P:(c + 1) * P], in1=nbias[:, h, :],
                                scale=1.0, scalar=3e38, op0=ALU.add, op1=ALU.min, accum_out=mn[:, c % 2, h:h + 1])
                        ins.then_inc(scored, 1)

                    def probs(c):
                        dve.wait_ge(t_filled, n * 4 + c + 1)
                        nc.vector.tensor_copy(pt[c % 2][:, :, :], PT_BANK[:, :].rearrange("p (h q) -> p h q", h=HG))\
                            .then_inc(pt_ready, 1)

                    def normalise(c):
                        dve.wait_ge(pv_filled, n * 4 + c + 1)
                        o = PV_BANK[:, 0:HG * (HD + 1)].rearrange("p (h d) -> p h d", h=HG)
                        nc.vector.reciprocal(ri[:, c % 2, :], o[:, :, HD]).then_inc(inverted, 1)
                        dve.wait_ge(inverted, n * 4 + c + 1)
                        tt(on[:, c, :, :], o[:, :, 0:HD], spread(ri[:, c % 2, :], 2, HD), ALU.mult).then_inc(on_ready, 1)

                    if tb == 0:
                        ts(nbias[:, :, :], nbias[:, :, :], 0.5, None, ALU.mult).then_inc(halved, 1)
                        dve.wait_ge(halved, g + 1)
                    dve.wait_ge(s_filled, n + 1)
                    nc.vector.memset(fence[:, :], 0.0)
                    score(0)
                    score(1)
                    probs(0)
                    score(2)
                    normalise(0)
                    probs(1)
                    score(3)
                    normalise(1)
                    probs(2)
                    if weights:
                        weights_low(it, k, WA, par_n, tb, g * 3 + tb)
                    normalise(2)
                    probs(3)
                    if weights:
                        weights_low(it, k, WB, par_n, tb, g * 3 + tb)
                    normalise(3)
                    if ahead:
                        leave_v_natural(it, k)

            both(dve, program)


TC = 256
NTC = TOK // TC
TT = TC // P
DT = DM // P


def output_stage(nc, sem, psum, ident, mean_w, h_dram, attn_dram, w_out, b_out, gate_w, base_w, base_b, lora_a, lora_b, out):
    R = Region(nc, "out_", X_AT, END_AT)
    wo_h, wo_l = R("w_out_high", [P, DK, DT, P], F32R), R("w_out_low", [P, DK, DT, P], F32R)
    wb_h, wb_l = R("base_high", [P, DK, DT, P], F32R), R("base_low", [P, DK, DT, P], F32R)
    la_h, la_l = R("lora_a_high", [P, DK, NE * RANK], F32R), R("lora_a_low", [P, DK, NE * RANK], F32R)
    lbT = R("lora_bT", [P, DT, P])
    g_h, g_l = R("gate_high", [P, DK, NE], F32R), R("gate_low", [P, DK, NE], F32R)
    bo, bb = R("b_out", [P, DT]), R("base_b", [P, DT])
    lg, m8 = R("logits", [P, TT, NE]), R("sorted", [P, TT, 8])
    tri = R("earlier", [P, NE, NE])
    pw, rank, wsel = R("pair_weights", [P, 4, TT]), R("rank", [P, TT * NE]), R("selected", [P, 2, TT, NE])
    fence = R("fence", [P, 1])
    cen_at = R.at
    atf = R("attended", [P, DK, TC])
    cen = nc.alloc_sbuf_tensor_at("out_centred", [P, DK, TC], F32, offset=cen_at)
    ah, al = R("att_high", [P, DK, TC], F32R), R("att_low", [P, DK, TC], F32R)
    hb = [R("h0", [P, DK, TC])]
    raws_at = R.at
    xh = R("norm_high", [P, DK, TC], F32R)
    sq_at = R.at
    xl = R("norm_low", [P, DK, TC], F32R)
    sq = nc.alloc_sbuf_tensor_at("out_squares", [P, DK, TC], F32, offset=sq_at)
    hb.append(R("h1", [P, DK, TC]))
    z = R("lora_low", [P, TC])
    y = [R(f"result{k}", [P, TC]) for k in range(2)]
    lgT = y[1][0:NE, :]
    ost = [R(f"result_natural{k}", [P, TT, 2 * P]) for k in range(2)]
    sums, rec = R("sums", [P, TC]), R("reciprocal", [P, TC])
    nwt = z
    cmp = rec[:, 0:P].rearrange("p (t e j) -> p t e j", t=TT, e=NE)
    eq = rec[:, P:2 * P].rearrange("p (t e j) -> p t e j", t=TT, e=NE)
    wx = rec[:, :].rearrange("p (t e r) -> p t e r", t=TT, e=NE)
    tt, ts, stt = nc.vector.tensor_tensor, nc.vector.tensor_scalar, nc.vector.scalar_tensor_tensor

    GATE, LOW, TURN, STATS = psum[2], psum[3], psum[4:6], psum[7]
    P_ACC = [psum[q] for q in (0, 1) * (DT // 2)]
    F_ACC = [psum[q] for q in (6, 0, 1, 6, 0, 1, 6, 1)]
    LOGITS = STATS[:, TC:TC + TT * NE]
    filled, freed = sem("oc_acc_filled"), sem("oc_acc_freed")

    def sum_features(source):
        return nc.vector.tensor_reduce(out=sums[:, :], in_=source[:, :, :].rearrange("p a t -> p t a"), axis=AX.X, op=ALU.add)

    W = Region(nc, "outw_", raws_at, END_AT)
    raw = [W(f"raw{k}", [P, DM]) for k in range(4)]
    raw_la, raw_lb, raw_g = W("raw_lora_a", [P, DM]), W("raw_lora_b", [P, DT, NE, RANK]), W("raw_gate", [NE, DM])
    raw_in = [sem(f"ow_raw_in{k}") for k in range(4)]
    small_in, turned, high, split = sem("ow_small_in"), sem("ow_turned"), sem("ow_high"), sem("ow_split")
    tri_made, lb_out = sem("ow_tri"), sem("ow_lb_out")
    att_in, first_in, att_high0 = [sem("ow_att_in0"), sem("ow_att_in1")], sem("ow_first_in"), sem("ow_att_high")
    att_low0, at_in = sem("ow_att_low"), sem("oc_attended_in")
    summed = sem("oc_summed")
    mats = ((w_out, wo_h, wo_l), (base_w, wb_h, wb_l))
    T_BANKS = psum[2:6]
    SMALL = DT * 4

    with nc.Block() as block:
        @block.sync
        def _(sp):
            for half in range(2):
                d = slice(half * (DK // 2), (half + 1) * (DK // 2))
                sp.dma_start(atf[:, d, :], attn_dram[d, :, 0:TC].rearrange("g p t -> p g t")).then_inc(att_in[half], 16)
            for it in range(DT // 2):
                for k in range(4):
                    sp.wait_ge(turned, it * 8 + 2 * k + 2)
                    sp.dma_start(raw[k][:, :], mats[k % 2][0][bass.ds((it * 2 + k // 2) * P, P), :]).then_inc(raw_in[k], 16)
                if it == 0:
                    sp.wait_ge(att_low0, 2)
                    sp.dma_start(atf[:, :, :], attn_dram[:, :, TC:2 * TC].rearrange("g p t -> p g t")).then_inc(at_in, 16)

        @block.gpsimd
        def _(pool):
            with nc.allow_non_contiguous_dma("small operands"):
                pool.dma_start(bo[:, :], b_out.rearrange("(t p) -> p t", p=P)).then_inc(first_in, 16)
                pool.dma_start(hb[0][:, :, :], h_dram[0].rearrange("p a c s -> p a (c s)")).then_inc(first_in, 16)
                pool.dma_start(raw_la[:, :], lora_a.rearrange("e r d -> (e r) d")).then_inc(small_in, 16)
                pool.dma_start(raw_g[:, :], gate_w).then_inc(small_in, 16)
                for e in range(NE):
                    pool.dma_start(raw_lb[:, :, e, :], lora_b[e].rearrange("(t p) r -> p t r", p=P)).then_inc(small_in, 16)
                pool.dma_start(bb[:, :], base_b.rearrange("(t p) -> p t", p=P)).then_inc(small_in, 16)
            nc.gpsimd.memset(tri[:, :, :], 1.0).then_inc(tri_made, 1)
            pool.wait_ge(tri_made, 1)
            nc.gpsimd.affine_select(out=tri[:, :, :], in_=tri[:, :, :], compare_op=ALU.is_gt, fill=0.0, base=0,
                                    pattern=[[1, NE], [-1, NE]], channel_multiplier=0).then_inc(tri_made, 1)
            pool.wait_ge(tri_made, 2)
            pool.wait_ge(at_in, 16)
            pool.wait_ge(small_in, 16 * (NE + 3))

        @block.tensor
        def _(pe):
            pe.sem_inc(turned, 8)
            for it in range(DT // 2):
                for q in range(2):
                    for k in (2 * q, 2 * q + 1):
                        pe.wait_ge(raw_in[k], it * 16 + 16)
                        for half in range(2):
                            pe.wait_ge(split, it * 8 + 2 * k + half + 1)
                            for d in range(DK // 2):
                                dk = half * (DK // 2) + d
                                ins = nc.tensor.transpose(T_BANKS[2 * (k % 2) + half][:, d * P:(d + 1) * P],
                                                          raw[k][:, dk * P:(dk + 1) * P], ident[:, :])
                            ins.then_inc(turned, 1)
                    pe.wait_ge(freed, it * 2 + q + 1)
                    for half in range(2):
                        pe.wait_ge(att_low0, half + 1)
                        pe.wait_ge(split, it * 8 + 4 * q + half + 5)
                        for m in range(half * 12, half * 12 + 12):
                            d, part = m // 3, m % 3
                            w, x = ((wo_l, ah), (wo_h, al), (wo_h, ah))[part]
                            ins = nc.tensor.matmul(P_ACC[q][:, 0:TC],
                                                   w[:, d, it * 2 + q, :],
                                                   x[:, d, :], start=(m == 0), stop=(m == 3 * DK - 1))
                    ins.then_inc(filled, 1)
            pe.wait_ge(small_in, 16 * (NE + 3))
            pe.wait_ge(split, SMALL + 4)
            for half in range(2):
                for d in range(DK // 2):
                    dk = half * (DK // 2) + d
                    ins = nc.tensor.transpose(psum[2 + half][:, d * P:(d + 1) * P], raw_la[:, dk * P:(dk + 1) * P], ident[:, :])
                ins.then_inc(turned, 1)
            for dk in range(DK):
                ins = nc.tensor.transpose(psum[4][:, dk * NE:(dk + 1) * NE], raw_g[:, dk * P:(dk + 1) * P],
                                          ident[0:NE, 0:NE])
            ins.then_inc(turned, 1)
            for half in range(2):
                for t in range(4):
                    ins = nc.tensor.transpose(psum[6 + half][:, t * P:(t + 1) * P],
                                              raw_lb[:, half * 4 + t, :, :], ident[:, :])
                ins.then_inc(turned, 1)

        def halves(h, l, k_half, it=None, k=None):
            d = slice(k_half * (DK // 2), (k_half + 1) * (DK // 2))
            if it is None:
                return h[:, d, :], l[:, d, :]
            at = bass.ds(it * 2 + k // 2, 1)
            return (h[:, d, at, :].rearrange("p d o q -> p d (o q)"), l[:, d, at, :].rearrange("p d o q -> p d (o q)"))

        def as_tiles(bank):
            return bank[:, 0:512].rearrange("p (d o) -> p d o", o=P)

        @block.scalar
        def _(act):
            for half in range(2):
                d = slice(half * (DK // 2), (half + 1) * (DK // 2))
                act.wait_ge(att_in[half], 16)
                nc.scalar.copy(ah[:, d, :], atf[:, d, :]).then_inc(att_high0, 1)
            for it in range(DT // 2):
                for k in range(4):
                    for half in range(2):
                        act.wait_ge(turned, it * 8 + 2 * k + half + 9)
                        nc.scalar.copy(halves(*mats[k % 2][1:], half, it, k)[0], as_tiles(T_BANKS[2 * (k % 2) + half]))\
                            .then_inc(high, 1)
            for half in range(2):
                act.wait_ge(turned, 8 + SMALL + half + 1)
                nc.scalar.copy(halves(la_h, la_l, half)[0], as_tiles(psum[2 + half])).then_inc(high, 1)
            act.wait_ge(turned, 8 + SMALL + 3)
            nc.scalar.copy(g_h[:, :, :], psum[4][:, 0:DK * NE].rearrange("p (d e) -> p d e", e=NE)).then_inc(high, 1)
            for half in range(2):
                act.wait_ge(turned, 8 + SMALL + 4 + half)
                nc.scalar.copy(lbT[:, half * 4:half * 4 + 4, :], as_tiles(psum[6 + half])).then_inc(lb_out, 1)

        @block.vector
        def _(dve):
            dve.sem_inc(split, 4)
            dve.sem_inc(freed, 2)
            for half in range(2):
                d = slice(half * (DK // 2), (half + 1) * (DK // 2))
                dve.wait_ge(att_high0, half + 1)
                tt(al[:, d, :], atf[:, d, :], ah[:, d, :].bitcast(F32), ALU.subtract).then_inc(att_low0, 1)

            for it in range(DT // 2):
                for q in range(2):
                    for k in (2 * q, 2 * q + 1):
                        for half in range(2):
                            dve.wait_ge(high, it * 8 + 2 * k + half + 1)
                            h, l = halves(*mats[k % 2][1:], half, it, k)
                            tt(l, as_tiles(T_BANKS[2 * (k % 2) + half]), h.bitcast(F32), ALU.subtract).then_inc(split, 1)
                    dve.wait_ge(filled, it * 2 + q + 1)
                    dve.wait_ge(first_in, 32)
                    at = bass.ds(it * 2 + q, 1)
                    h2 = hb[0][:, at, :].rearrange("p o t -> p (o t)")
                    stt(h2, P_ACC[q][:, 0:TC], bo[:, at], h2, ALU.add, ALU.add).then_inc(freed, 1)
            dve.wait_ge(freed, DT + 2)
            sum_features(hb[0]).then_inc(summed, 1)
            for half in range(2):
                dve.wait_ge(high, SMALL + half + 1)
                h, l = halves(la_h, la_l, half)
                tt(l, as_tiles(psum[2 + half]), h.bitcast(F32), ALU.subtract).then_inc(split, 1)
            dve.wait_ge(high, SMALL + 3)
            tt(g_l[:, :, :], psum[4][:, 0:DK * NE].rearrange("p (d e) -> p d e", e=NE), g_h[:, :, :].bitcast(F32),
               ALU.subtract).then_inc(split, 1)

    h_in = [sem("oc_h_in0"), sem("oc_h_in1")]
    a_high, a_low, a_low_1 = sem("oc_att_high"), sem("oc_att_low"), sem("oc_att_low_dve")
    averaged, centred, squared, rooted, nstep = sem("oc_averaged"), sem("oc_centred"), sem("oc_squared"), sem("oc_rooted"), sem("oc_newton")
    scaled, x_high, x_low_p, x_low_d = sem("oc_scaled"), sem("oc_norm_high"), sem("oc_norm_low_pool"), sem("oc_norm_low_dve")
    gated, gate_out, gate_turned, low_f, low_out = sem("oc_gated"), sem("oc_gate_out"), sem("oc_gate_turned"), sem("oc_low_filled"), sem("oc_low_out")
    gstep, diff, expd, wx_ready, wx_turned, z_ready = sem("oc_gate_steps"), sem("oc_diff"), sem("oc_exp"), sem("oc_weights_ready"), sem("oc_weights_turned"), sem("oc_z_ready")
    turned, turn_free = sem("oc_turned"), sem("oc_turn_freed")
    stored = [sem("oc_stored0"), sem("oc_stored1")]
    ITER = NTC // 2
    GATE_STEPS = 12

    def both(eng, program):
        with eng.Fori(0, ITER - 1) as it:
            program(it, False)
        program(ITER - 1, True)

    with nc.Block() as block:
        @block.sync
        def _(sp):
            def load_h(b, slot, half):
                d = slice(half * (DK // 2), (half + 1) * (DK // 2))
                sp.dma_start(hb[slot][:, d, :], h_dram[bass.ds(b, 1), :, d, :, :].rearrange("o p a c s -> p (o a) (c s)"))\
                    .then_inc(h_in[half], 16)

            load_h(1, 1, 0)
            load_h(1, 1, 1)

            def program(it, final):
                for k in range(2):
                    b = it * 2 + k
                    if not final:
                        sp.wait_ge(x_low_p, b + 1)
                        sp.wait_ge(x_low_d, b + 1)
                        sp.dma_start(atf[:, :, :], attn_dram[:, :, bass.ds(b * TC + 2 * TC, TC)].rearrange("g p t -> p g t"))\
                            .then_inc(at_in, 16)
                    for pair in range(DT // 2):
                        if not final and pair % 2 == 0 and pair:
                            sp.wait_ge(freed, b * (2 * DT) + 2 * DT + 4 + 2)
                            load_h(b + 2, k, 0)
                        sp.wait_ge(turn_free, b * (DT // 2) + pair + 3)
                        sp.dma_start(out[bass.ds(b * TC, TC), pair * 2 * P:(pair + 1) * 2 * P]
                                     .rearrange("(t p) o -> p t o", p=P), ost[pair % 2][:, :, :]).then_inc(stored[pair % 2], 16)
                    if not final:
                        load_h(b + 2, k, 1)

            both(sp, program)
            for q in range(2):
                sp.wait_ge(stored[q], 16 * (NTC * DT // 4 + 1))

        @block.tensor
        def _(pe):
            def project(r, ot):
                pe.wait_ge(freed, r + 1)
                for m in range(3 * DK):
                    d, part = m // 3, m % 3
                    w, x = ((wo_l, ah), (wo_h, al), (wo_h, ah))[part]
                    ins = nc.tensor.matmul(P_ACC[ot][:, 0:TC], w[:, d, ot, :], x[:, d, :], start=(m == 0),
                                           stop=(m == 3 * DK - 1))
                ins.then_inc(filled, 1)

            def feed_forward(r, ot, a=0, b=3 * DK):
                if a == 0:
                    pe.wait_ge(freed, r if 0 < ot < DT - 1 else r + 1)
                for m in range(a, b):
                    d, part = m // 3, m % 3
                    w, x = ((wb_l, xh), (wb_h, xl), (wb_h, xh))[part]
                    nc.tensor.matmul(F_ACC[ot][:, 0:TC], w[:, d, ot, :], x[:, d, :], start=(m == 0), stop=False)

            def average(source, count):
                pe.wait_ge(summed, count)
                nc.tensor.matmul(STATS[:, 0:TC], mean_w[:, :], source[:, :], start=True, stop=True).then_inc(averaged, 1)

            pe.sem_inc(turned, 2)
            average(sums, 1)
            pe.wait_ge(a_low_1, 1)

            def program(it, final):
                for k in range(2):
                    b = it * 2 + k
                    ahead = not (final and k == 1)
                    r0 = b * (2 * DT) + DT
                    if ahead:
                        pe.wait_ge(a_low, b + 2)
                        for ot in range(3):
                            project(r0 + ot, ot)
                    average(sums, b * 2 + 2)
                    if ahead:
                        for ot in range(3, DT):
                            project(r0 + ot, ot)
                        r0 = r0 + DT
                    pe.wait_ge(x_low_p, b + 1)
                    pe.wait_ge(x_low_d, b + 1)
                    for bank, w_h, w_l, done in ((GATE[0:NE, 0:TC], g_h, g_l, gated), (LOW[:, 0:TC], la_h, la_l, low_f)):
                        for m in range(3 * DK):
                            d, part = m // 3, m % 3
                            w, x = ((w_l, xh), (w_h, xl), (w_h, xh))[part]
                            if done is low_f and m == 2 * DK:
                                pe.wait_ge(gate_out, b + 1)
                            ins = nc.tensor.matmul(bank, w[:, d, :], x[:, d, :], start=(m == 0), stop=(m == 3 * DK - 1))
                        ins.then_inc(done, 1)
                    for t in range(TT):
                        ins = nc.tensor.transpose(LOGITS[:, t * NE:(t + 1) * NE], lgT[:, t * P:(t + 1) * P],
                                                  ident[0:NE, 0:NE])
                    ins.then_inc(gate_turned, 1)

                    def lora(ot):
                        nc.tensor.matmul(F_ACC[ot][:, 0:TC], lbT[:, ot, :], z[:, :], start=False, stop=True).then_inc(filled, 1)

                    def turn(ot):
                        pe.wait_ge(freed, r0 + ot + 3)
                        if ot % 2 == 0:
                            pe.wait_ge(turn_free, b * (DT // 2) + ot // 2 + 1)
                        for t in range(TT):
                            ins = nc.tensor.transpose(TURN[ot // 2 % 2][:, t * 2 * P + (ot % 2) * P:t * 2 * P + (ot % 2 + 1) * P],
                                                      y[ot % 2][:, t * P:(t + 1) * P], ident[:, :])
                        ins.then_inc(turned, 1)

                    feed_forward(r0, 0)
                    feed_forward(r0 + 1, 1, 0, 18)
                    pe.wait_ge(wx_ready, b + 1)
                    for t in range(TT):
                        ins = nc.tensor.transpose(GATE[:, TC + t * P:TC + (t + 1) * P], rec[:, t * P:(t + 1) * P], ident[:, :])
                    ins.then_inc(wx_turned, 1)
                    feed_forward(r0 + 1, 1, 18)
                    pe.wait_ge(z_ready, b + 1)
                    lora(0)
                    lora(1)
                    for ot in range(2, DT):
                        feed_forward(r0 + ot, ot)
                        lora(ot)
                        turn(ot - 2)
                        if ot == 4 and ahead:
                            average(sums, b * 2 + 3)
                    turn(DT - 2)
                    turn(DT - 1)

            both(pe, program)

        @block.scalar
        def _(act):
            act.sem_inc(turn_free, 2)
            act.sem_inc(stored[0], 16)
            act.sem_inc(stored[1], 16)

            def att_high(b):
                act.wait_ge(at_in, b * 16)
                nc.scalar.copy(ah[:, :, :], atf[:, :, :]).then_inc(a_high, 1)

            act.sem_inc(a_high, 1)
            att_high(1)

            def program(it, final):
                for k in range(2):
                    b = it * 2 + k
                    ahead = not (final and k == 1)
                    act.wait_ge(centred, b + 1)
                    nc.scalar.activation(sq[:, :, :], cen[:, :, :], ACT.Square).then_inc(squared, 1)
                    act.wait_ge(averaged, b * 2 + 2)
                    nc.scalar.activation(rec[:, :], STATS[:, 0:TC], ACT.Sqrt, bias=LN_EPS).then_inc(rooted, 1)
                    act.wait_ge(scaled, b + 1)
                    nc.scalar.copy(xh[:, :, :], cen[:, :, :]).then_inc(x_high, 1)
                    act.wait_ge(gated, b + 1)
                    nc.scalar.copy(lgT[:, :], GATE[0:NE, 0:TC]).then_inc(gate_out, 1)
                    act.wait_ge(diff, b + 1)
                    nc.scalar.activation(pw[:, 1, :], pw[:, 0, :], ACT.Exp).then_inc(expd, 1)
                    act.wait_ge(low_f, b + 1)
                    nc.scalar.copy(z[:, :], LOW[:, 0:TC]).then_inc(low_out, 1)
                    for pair in range(DT // 2):
                        if pair == 1 and not final:
                            att_high(b + 2)
                        act.wait_ge(turned, b * DT + 2 * pair + 4)
                        act.wait_ge(stored[pair % 2], (b * 2 + pair // 2) * 16 + 16)
                        nc.scalar.copy(ost[pair % 2][:, :, :], TURN[pair % 2][:, 0:512].rearrange("p (t o) -> p t o", t=TT))\
                            .then_inc(turn_free, 1)

            both(act, program)

        @block.gpsimd
        def _(pool):
            def att_low(b, d=slice(0, DK)):
                pool.wait_ge(a_high, b + 1)
                nc.gpsimd.tensor_tensor(out=al[:, d, :], in0=atf[:, d, :], in1=ah[:, d, :].bitcast(F32),
                                        op=ALU.subtract).then_inc(a_low, 1)

            pool.sem_inc(a_low, 1)
            att_low(1, slice(0, DK // 2))

            def program(it, final):
                for k in range(2):
                    b = it * 2 + k
                    pool.wait_ge(x_high, b + 1)
                    d = slice(DK // 2, DK)
                    nc.gpsimd.tensor_tensor(out=xl[:, d, :], in0=cen[:, d, :], in1=xh[:, d, :].bitcast(F32),
                                            op=ALU.subtract).then_inc(x_low_p, 1)
                    if not final:
                        att_low(b + 2)

            both(pool, program)

        @block.vector
        def _(dve):
            def leave_projection(r, slot, ot, half_in):
                dve.wait_ge(filled, r + 1)
                if half_in is not None:
                    dve.wait_ge(h_in[ot // (DT // 2)], half_in)
                stt(hb[slot][:, ot, :], P_ACC[ot][:, 0:TC], bo[:, ot:ot + 1], hb[slot][:, ot, :], ALU.add, ALU.add)\
                    .then_inc(freed, 1)

            dve.wait_ge(a_high, 2)
            d = slice(DK // 2, DK)
            tt(al[:, d, :], atf[:, d, :], ah[:, d, :].bitcast(F32), ALU.subtract).then_inc(a_low_1, 1)
            dve.wait_ge(a_low_1, 1)

            def program(it, final):
                for k in range(2):
                    b = it * 2 + k
                    ahead = not (final and k == 1)
                    r0 = b * (2 * DT) + DT
                    nxt = 1 - k

                    def project_out(ot):
                        if ahead:
                            leave_projection(r0 + ot, nxt, ot, (b + 1) * 16 if ot % (DT // 2) == 0 else None)

                    dve.wait_ge(averaged, b * 2 + 1)
                    if ahead:
                        dve.wait_ge(a_low, b + 2)
                    tt(cen[:, :, :], hb[k][:, :, :], spread(STATS[:, 0:TC], 1, DK), ALU.subtract).then_inc(centred, 1)
                    project_out(0)
                    dve.wait_ge(squared, b + 1)
                    sum_features(sq).then_inc(summed, 1)
                    project_out(1)
                    project_out(2)
                    dve.wait_ge(rooted, b + 1)
                    base = b * 5
                    nc.vector.reciprocal(rec[:, :], rec[:, :]).then_inc(nstep, 1)
                    dve.wait_ge(nstep, base + 1)
                    tt(nwt[:, :], rec[:, :], rec[:, :], ALU.mult).then_inc(nstep, 1)
                    dve.wait_ge(nstep, base + 2)
                    stt(nwt[:, :], STATS[:, 0:TC], LN_EPS, nwt[:, :], ALU.add, ALU.mult).then_inc(nstep, 1)
                    dve.wait_ge(nstep, base + 3)
                    ts(nwt[:, :], nwt[:, :], -0.5, 1.5, ALU.mult, ALU.add).then_inc(nstep, 1)
                    dve.wait_ge(nstep, base + 4)
                    tt(rec[:, :], rec[:, :], nwt[:, :], ALU.mult).then_inc(nstep, 1)
                    project_out(3)
                    dve.wait_ge(nstep, base + 5)
                    tt(cen[:, :, :], cen[:, :, :], spread(rec[:, :], 1, DK), ALU.mult).then_inc(scaled, 1)
                    project_out(4)
                    project_out(5)
                    dve.wait_ge(x_high, b + 1)
                    d = slice(0, DK // 2)
                    tt(xl[:, d, :], cen[:, d, :], xh[:, d, :].bitcast(F32), ALU.subtract).then_inc(x_low_d, 1)
                    project_out(6)
                    project_out(7)
                    if ahead:
                        r0 = r0 + DT
                        dve.wait_ge(freed, r0 + 2)
                        sum_features(hb[nxt]).then_inc(summed, 1)

                    steps = [0]

                    def link(ins):
                        steps[0] += 1
                        ins.then_inc(gstep, 1)
                        dve.wait_ge(gstep, b * GATE_STEPS + steps[0])

                    dve.wait_ge(gate_turned, b + 1)
                    link(nc.vector.tensor_copy(lg[:, :, :], LOGITS.rearrange("p (t e) -> p t e", e=NE)))
                    nc.vector.memset(fence[:, :], 0.0)
                    for t in range(TT):
                        ins = nc.vector.max(m8[:, t, :], lg[:, t, :])
                        if t == TT - 1:
                            link(ins)
                    tt(pw[:, 0, :], m8[:, :, 1], m8[:, :, 0], ALU.subtract).then_inc(diff, 1)
                    tt(cmp, spread(lg[:, :, :], 2, NE), spread(lg[:, :, :], 3, NE), ALU.is_gt)
                    link(tt(eq, spread(lg[:, :, :], 2, NE), spread(lg[:, :, :], 3, NE), ALU.is_equal))
                    link(tt(eq, eq, spread(tri[:, :, :], 1, TT), ALU.mult))
                    link(tt(cmp, cmp, eq, ALU.add))
                    link(nc.vector.tensor_reduce(out=rank[:, :], in_=cmp, axis=AX.X, op=ALU.add))
                    dve.wait_ge(expd, b + 1)
                    link(ts(pw[:, 2, :], pw[:, 1, :], 1.0, None, ALU.add))
                    link(nc.vector.reciprocal(pw[:, 2, :], pw[:, 2, :]))
                    link(tt(pw[:, 3, :], pw[:, 1, :], pw[:, 2, :], ALU.mult))
                    for q in range(2):
                        ins = stt(wsel[:, q, :, :], rank[:, :].rearrange("p (t e) -> p t e", e=NE), float(q),
                                  spread(pw[:, 2 + q, :], 2, NE), ALU.is_equal, ALU.mult)
                        link(ins)
                    link(ts(wsel[:, :, :, :], wsel[:, :, :, :], LORA_SCALE, None, ALU.mult))
                    tt(wx, spread(wsel[:, 0, :, :], 3, RANK), spread(wsel[:, 1, :, :], 3, RANK), ALU.add).then_inc(wx_ready, 1)
                    assert steps[0] == GATE_STEPS
                    dve.wait_ge(low_out, b + 1)
                    dve.wait_ge(wx_turned, b + 1)
                    tt(z[:, :], z[:, :], GATE[:, TC:2 * TC], ALU.mult).then_inc(z_ready, 1)
                    for ot in range(DT):
                        dve.wait_ge(filled, r0 + ot + 1)
                        dve.wait_ge(turned, b * DT + ot + 1)
                        stt(y[ot % 2][:, :], F_ACC[ot][:, 0:TC], bb[:, ot:ot + 1], hb[k][:, ot, :], ALU.add, ALU.add)\
                            .then_inc(freed, 1)

            both(dve, program)


def program(nc, x, log_dt, b_ri, inv_a, a_imag, w_qkv, b_qkv, w_out, b_out, gate_w, base_w, base_b, lora_a, lora_b,
            out, h_dram, attn_dram):
    def sem(name):
        return nc.alloc_semaphore(name)

    psum = [nc.alloc_psum_tensor(f"bank{k}", [P, 512], F32) for k in range(8)]
    CR = Region(nc, "const_", CONST_AT, CONST_AT + CONST_BYTES)
    ident, mean_w = CR("ident", [P, P]), CR("mean_w", [P, P])
    H = nc.alloc_sbuf_tensor_at("h", [P, DK, BATCH, SEQ], F32, offset=H_AT)
    means = nc.alloc_sbuf_tensor_at("h_mean", [P, BATCH, SEQ], F32, offset=T_AT)
    XH = nc.alloc_sbuf_tensor_at("x_high", [P, DK, TOK], F32R, offset=X_AT)
    XL = nc.alloc_sbuf_tensor_at("x_low", [P, DK, TOK], F32R, offset=X_AT + X_BYTES // 2)
    constants(nc, sem, ident, mean_w)
    s4d_stage(nc, sem, psum, x, log_dt, b_ri, inv_a, a_imag, ident, mean_w, H, means)
    QKV = Region(nc, "qkv_", H_AT, END_AT)
    wh = [QKV(f"w_high{k}", [P, 3, DK, P], F32R) for k in range(2)]
    wl = [QKV(f"w_low{k}", [P, 3, DK, P], F32R) for k in range(2)]
    norm_stage(nc, sem, psum, ident, mean_w, H, means, XH, XL, wh[0], wl[0], w_qkv, h_dram)
    attention_stage(nc, sem, psum, ident, XH, XL, wh, wl, w_qkv, b_qkv, attn_dram)
    output_stage(nc, sem, psum, ident, mean_w, h_dram, attn_dram, w_out, b_out, gate_w, base_w, base_b, lora_a, lora_b,
                 out.rearrange("b s o -> (b s) o"))


_INS = ["x", "L0_tok_log_dt", "L0_tok_B", "L0_tok_inv_A_real", "L0_tok_A_imag", "L0_attn_w_qkv", "L0_attn_b_qkv",
        "L0_attn_w_out", "L0_attn_b_out", "L0_ffn_gate_w", "L0_ffn_base_w", "L0_ffn_base_b", "L0_ffn_lora_A",
        "L0_ffn_lora_B"]


def kernel(**inputs):
    import concourse.bacc as _bacc
    from concourse.bass_utils import run_bass_kernel_spmd as _run

    nc = _bacc.Bacc("TRN2", target_bir_lowering=False, num_devices=1)
    arrays, args = {}, []
    for name in _INS:
        a = np.ascontiguousarray(inputs[name])
        arrays[f"in_{name}"] = a
        args.append(nc.dram_tensor(f"in_{name}", list(a.shape), mybir.dt.from_np(a.dtype), kind="ExternalInput").ap())
    args.append(nc.dram_tensor("out", [BATCH, SEQ, DM], F32, kind="ExternalOutput").ap())
    args.append(nc.dram_tensor("h_scratch", [NTC, P, DK, TC // SEQ, SEQ], F32, kind="Internal").ap())
    args.append(nc.dram_tensor("attended_scratch", [NG, P, TOK], F32, kind="Internal").ap())
    program(nc, *args)
    r = _run(nc, [arrays], core_ids=[0])
    return r.results[0]["out"]
```
